# Optimizing a Trainium2 kernel written in Bass

```python
import numpy as np
import jax
import jax.numpy as jnp

def _softmax(x, axis=-1):
    return jax.nn.softmax(x, axis=axis)

def _gelu(x):
    return jax.nn.gelu(x, approximate=True)

def _silu(x):
    return jax.nn.silu(x)

def _sigmoid(x):
    return jax.nn.sigmoid(x)

def _layernorm(x, axis=-1, eps=1e-05):
    m = jnp.mean(x, axis=axis, keepdims=True)
    v = jnp.var(x, axis=axis, keepdims=True)
    return (x - m) / jnp.sqrt(v + eps)

def _scatter_add(tgt, idx, src, axis=0):
    return tgt.at[idx].add(src)

def _segment_sum(src, seg, n):
    return jax.ops.segment_sum(src, seg, n)
kernel_name = 'mk_decoder_preln_d1_seqx_r8_5a7c8f'

def setup_inputs(seed: int=0):
    np.random.seed(seed)
    _w = jnp.asarray

    def _rec_inputs():
        import jax
        import jax.numpy as jnp
        _rk = jax.random.key(seed)
        x = -0.0003929 + 0.9999 * jax.random.normal(jax.random.fold_in(_rk, 1), (64, 128, 128), jnp.float32)
        _lenS = 128 - jax.random.randint(jax.random.fold_in(_rk, 7), (64,), 0, max(1, 128 // 4) + 1, jnp.int32)
        _lenS2 = 120 - jax.random.randint(jax.random.fold_in(_rk, 8), (64,), 0, max(1, 120 // 4) + 1, jnp.int32)
        _ctx_1024P = jax.random.normal(jax.random.fold_in(_rk, 11), (64, 16, 128), jnp.float32)
        _ctx_1024c = jax.random.dirichlet(jax.random.fold_in(_rk, 511), 0.3 * jnp.ones((16,), jnp.float32), (64, 120))
        _ctx_1024t = jnp.einsum('bsk,bkd->bsd', _ctx_1024c, _ctx_1024P)
        _ctx_1024t = _ctx_1024t * jax.lax.rsqrt(jnp.mean(jnp.square(_ctx_1024t)) + 1e-12) * 0.953939
        ctx_1024 = -1.39393e-06 + 0.999914 * (_ctx_1024t + 0.3 * jax.random.normal(jax.random.fold_in(_rk, 611), (64, 120, 128), jnp.float32))
        _validS = jnp.arange(128)[None, :] < _lenS[:, None]
        _validS2 = jnp.arange(120)[None, :] < _lenS2[:, None]
        _causal = jnp.tril(jnp.ones((128, 128), dtype=bool))
        mask_BxS2_ik0 = jnp.where(jnp.broadcast_to(_validS2[:, :], (64, 120)), 0, 1).astype(jnp.int32)
        return (x, ctx_1024, mask_BxS2_ik0)
    x, ctx_1024, mask_BxS2_ik0 = _rec_inputs()

    def _L0_attn_setup():
        import jax, jax.numpy as jnp
        import numpy as np
        DIM = 128
        B, T = (4, 1024)
        key = jax.random.key(seed)
        ks = jax.random.split(key, 5)
        scale = 1.0 / np.sqrt(DIM)
        x = jax.random.normal(ks[0], (B, T, DIM), dtype=jnp.float32)
        w_in = jax.random.uniform(ks[1], (DIM, DIM), jnp.float32, -scale, scale)
        b_in = jax.random.uniform(ks[2], (DIM,), jnp.float32, -scale, scale)
        a = jnp.zeros((DIM,), jnp.float32)
        b = jnp.ones((DIM,), jnp.float32)
        w_out = jax.random.uniform(ks[3], (DIM, DIM), jnp.float32, -scale, scale)
        b_out = jax.random.uniform(ks[4], (DIM,), jnp.float32, -scale, scale)
        return {'x': x, 'w_in': w_in, 'b_in': b_in, 'a': a, 'b': b, 'w_out': w_out, 'b_out': b_out}
    _L0_attn_all = _L0_attn_setup()
    _L0_attn_in = {k: v for k, v in _L0_attn_all.items() if k in ('w_in', 'b_in', 'a', 'b', 'w_out', 'b_out')}
    del _L0_attn_all

    def _L0_xattn_setup():
        import jax, jax.numpy as jnp
        import numpy as np
        B, P, Q, H = (8, 256, 64, 128)
        key = jax.random.key(seed)
        k1, k2, k3, k4, k5 = jax.random.split(key, 5)
        passage = jax.random.normal(k1, (B, P, H), dtype=jnp.float32)
        question = jax.random.normal(k2, (B, Q, H), dtype=jnp.float32)
        q_mask = jax.random.randint(k3, (B, Q), 0, 2, dtype=jnp.int32)
        bound = 1.0 / np.sqrt(H)
        map_W = jax.random.uniform(k4, (H, H), jnp.float32, -bound, bound)
        map_b = jax.random.uniform(k5, (H,), jnp.float32, -bound, bound)
        return {'passage': passage, 'question': question, 'q_mask': q_mask, 'map_W': map_W, 'map_b': map_b}
    _L0_xattn_all = _L0_xattn_setup()
    _L0_xattn_in = {k: v for k, v in _L0_xattn_all.items() if k in ('map_W', 'map_b')}
    del _L0_xattn_all

    def _L0_ffn_setup():
        import jax, jax.numpy as jnp
        import numpy as np
        CAPACITY_RATIO = 0.75
        key = jax.random.key(seed)
        k1, k2, k3 = jax.random.split(key, 3)
        B, L, D = (4, 1024, 128)
        x = jax.random.normal(k1, (B, L, D), dtype=jnp.float32)
        w_router = jax.random.normal(k2, (D,), dtype=jnp.float32) * 0.02
        w_block = jax.random.normal(k3, (D, D), dtype=jnp.float32) * 0.02
        return {'x': x, 'w_router': w_router, 'w_block': w_block}
    _L0_ffn_all = _L0_ffn_setup()
    _L0_ffn_in = {k: v for k, v in _L0_ffn_all.items() if k in ('w_router', 'w_block')}
    del _L0_ffn_all
    return {'x': x, 'ctx_1024': ctx_1024, 'mask_BxS2_ik0': mask_BxS2_ik0, 'L0_attn_w_in': _L0_attn_in['w_in'], 'L0_attn_b_in': _L0_attn_in['b_in'], 'L0_attn_a': _L0_attn_in['a'], 'L0_attn_b': _L0_attn_in['b'], 'L0_attn_w_out': _L0_attn_in['w_out'], 'L0_attn_b_out': _L0_attn_in['b_out'], 'L0_xattn_map_W': _L0_xattn_in['map_W'], 'L0_xattn_map_b': _L0_xattn_in['map_b'], 'L0_ffn_w_router': _L0_ffn_in['w_router'], 'L0_ffn_w_block': _L0_ffn_in['w_block']}

def reference(x, ctx_1024, mask_BxS2_ik0, L0_attn_w_in, L0_attn_b_in, L0_attn_a, L0_attn_b, L0_attn_w_out, L0_attn_b_out, L0_xattn_map_W, L0_xattn_map_b, L0_ffn_w_router, L0_ffn_w_block):
    import jax
    import jax.numpy as jnp

    def _L0_attn_ref(x, w_in, b_in, a, b, w_out, b_out):
        import jax, jax.numpy as jnp
        import numpy as np
        DIM = 128
        B, T = (4, 1024)
        h = jnp.einsum('btd,ed->bte', x, w_in) + b_in
        A = jax.nn.sigmoid(a)

        def step(state, h_t):
            state = A * state + b * h_t
            return (state, state)
        init = jnp.zeros_like(h[:, 0])
        _, ys = jax.lax.scan(step, init, jnp.swapaxes(h, 0, 1))
        y = jnp.swapaxes(ys, 0, 1)
        return jnp.einsum('btd,ed->bte', y, w_out) + b_out

    def _L0_xattn_ref(passage, question, q_mask, map_W, map_b):
        import jax, jax.numpy as jnp
        import numpy as np
        B, P, Q, H = (8, 256, 64, 128)
        scores = jnp.einsum('bph,bqh->bpq', passage, question)
        mask = q_mask.astype(scores.dtype)[:, None, :]
        a = jax.nn.softmax(scores * mask, axis=-1) * mask
        alpha = a / (jnp.sum(a, axis=-1, keepdims=True) + 1e-13)
        out = jnp.einsum('bpq,bqh->bph', alpha, question)
        return jax.nn.relu(jnp.einsum('bph,oh->bpo', out, map_W) + map_b)

    def _L0_ffn_ref(x, w_router, w_block):
        import jax, jax.numpy as jnp
        import numpy as np
        CAPACITY_RATIO = 0.75
        B, L, D = x.shape
        k = max(1, int(L * CAPACITY_RATIO))
        scores = jnp.einsum('bld,d->bl', x, w_router)
        _, top_idx = jax.lax.top_k(scores, k)
        selected = jnp.take_along_axis(x, top_idx[:, :, None], axis=1)
        processed = jax.nn.gelu(jnp.einsum('bkd,de->bke', selected, w_block))
        batch_idx = jnp.arange(B)[:, None]
        out = x.at[batch_idx, top_idx].set(processed)
        return out
    x = x + _L0_attn_ref(_layernorm(x, axis=-1), L0_attn_w_in, L0_attn_b_in, L0_attn_a, L0_attn_b, L0_attn_w_out, L0_attn_b_out)
    x = x + _L0_xattn_ref(_layernorm(x, axis=-1), ctx_1024, mask_BxS2_ik0, L0_xattn_map_W, L0_xattn_map_b)
    x = x + _L0_ffn_ref(_layernorm(x, axis=-1), L0_ffn_w_router, L0_ffn_w_block)
    return x

_drawn_inputs = setup_inputs


def setup_inputs(seed=0):
    import zlib

    import numpy as np

    out = dict(_drawn_inputs(seed))
    spreads = {'L0_attn_a': (0.0, 0.1), 'L0_attn_b': (1.0, 0.2)}
    factors = {}
    for name, (base, spread) in spreads.items():
        noise = np.random.default_rng([zlib.crc32(name.encode()), seed]).standard_normal(out[name].shape)
        drawn = base * np.exp(spread * noise) if base else spread * noise
        out[name] = jnp.asarray(drawn.astype(out[name].dtype))
    for name, factor in factors.items():
        out[name] = (out[name] * factor).astype(out[name].dtype)
    return out
```

```python
from contextlib import ExitStack

import concourse.bass as bass
from concourse import mybir

F32 = mybir.dt.float32
BF16 = mybir.dt.bfloat16
I32 = mybir.dt.int32
ALU = mybir.AluOpType
ACT = mybir.ActivationFunctionType
AX_X = mybir.AxisListType.X

P = 128
J = 4
U = 2
EPS = 1e-5
TINY = 1e-13
LOWEST = -3.0e38
CAPACITY = 0.75


def decoder_layer(nc: bass.Bass, x, ctx, mask, w_in, b_in, a, b, w_out, b_out, map_W, map_b, w_router, w_block, out):
    B, S, D = x.shape
    Q = ctx.shape[1]
    NG = B // J
    DROP = S - max(1, int(S * CAPACITY))
    ROUNDS = DROP // 8
    assert S == P and D == P and B % (J * U) == 0 and DROP % 8 == 0
    FIRST, LAST = -1, NG + 3
    LOOP0, LOOP1 = 5, NG - 1
    assert (LOOP1 - LOOP0) % U == 0 and LOOP1 - LOOP0 > 0

    x_dram = x.rearrange("(g j) t d -> g t j d", j=J)
    ctx_dram = ctx.rearrange("(g j) q d -> g q j d", j=J)
    out_dram = out.rearrange("(g j) t d -> g t j d", j=2 * J)

    with ExitStack() as stack:
        def sb(name, shape, dt=F32):
            return stack.enter_context(nc.sbuf_tensor(name, shape, dt))

        def ps(name, shape):
            return stack.enter_context(nc.psum_tensor(name, shape, F32))

        def sem(name):
            return stack.enter_context(nc.semaphore(name))

        ident = sb("ident", [P, P])
        flip = sb("flip", [P, P])
        w_nat = sb("w_nat", [P, 3, P])
        w_inT = sb("w_inT", [P, P])
        w_outT = sb("w_outT", [P, P])
        mapWT = sb("mapWT", [P, P])
        block_in = sb("block_in", [P, P + 1])
        cols = sb("cols", [P, 2])
        decay = sb("decay", [P, 2])
        decay_row = sb("decay_row", [P, J, S])
        mapb_all = sb("mapb_all", [P, P])
        eps_col = sb("eps_col", [P, 1])
        mask_int = sb("mask_int", [B, Q], I32)
        mask_nat = sb("mask_nat", [B, Q])
        maskT = sb("maskT", [Q, B])
        mask_tiny = sb("mask_tiny", [Q, B])
        bias_row = sb("bias_row", [65, 3, P])
        bias_rest = sb("bias_rest", [65, 2, P])
        bias_hi = sb("bias_hi", [65, 2, P], BF16)
        bias_mid = sb("bias_mid", [65, 2, P], BF16)
        bias_parts = sb("bias_parts", [65, 2, P], BF16)
        bout_parts = sb("bout_parts", [65, J, P], BF16)
        ones_bf = sb("ones_bf", [65, J * S], BF16)

        x_in = sb("x_in", [P, U, J, D])
        c_in = sb("c_in", [Q, U, J, D])
        c_masked = sb("c_masked", [Q, U, J, D])
        c_maskedT = sb("c_maskedT", [P, U, J, Q])
        xn1 = sb("xn1", [P, U, J, D])
        xn1T = sb("xn1T", [P, U, J, S])
        yT = sb("yT", [P, U, J, S])
        xn2 = sb("xn2", [P, U, J, D])
        xn2T = sb("xn2T", [P, U, J, S])
        probs = sb("probs", [P, U, J, Q])
        probsT = sb("probsT", [Q, U, J, S])
        c_mapped = sb("c_mapped", [Q, U, J, D + 1])
        att = sb("att", [P, U, J, D])
        xn3 = sb("xn3", [P, U, J, D])
        xn3T = sb("xn3T", [P, U, J, S])
        bn1 = sb("bn1", [P, U, J, 6])
        bn2 = sb("bn2", [P, U, J, 6])
        bn3 = sb("bn3", [P, U, J, 6])
        mva = sb("mva", [P, U, 2 * J, 2])
        lna = sb("lna", [P, U, 2 * J])
        ya = sb("ya", [P, U, 2 * J])
        ta = sb("ta", [P, U, 2, 2 * J])
        ra = sb("ra", [P, U, 2 * J])
        na = sb("na", [P, U, 2 * J])
        mvb = sb("mvb", [P, U, J, 2])
        lnb = sb("lnb", [P, U, J])
        yb = sb("yb", [P, U, J])
        tb = sb("tb", [P, U, 2, J])
        rb = sb("rb", [P, U, J])
        nb = sb("nb", [P, U, J])
        negmax = sb("negmax", [P, U, J])
        inv = sb("inv", [P, U, J])

        xs = sb("xs", [P, NG, J, D])
        xn3_all = sb("xn3_all", [P, NG, J, D])
        gate = sb("gate", [P, NG, J, D + 1])
        score = sb("score", [P, B])
        ranked = sb("ranked", [B, S])
        top8 = sb("top8", [B, 8])
        dropped = sb("dropped", [B, S])
        droppedT = sb("droppedT", [P, B])

        tr = [ps("tr0", [P, 512]), ps("tr1", [P, 512])]
        h_ps = ps("h_ps", [P, J, S])
        o_ps = ps("o_ps", [P, J, D])
        s_ps = ps("s_ps", [P, 512])
        m_ps = ps("m_ps", [P, J, D])
        wide = ps("wide", [P, 2, 512])
        s_view = s_ps[:, 0:J * Q].rearrange("p (j q) -> p j q", j=J)
        wide_view = wide[:, :, 0:2 * (D + 1)].rearrange("p h (j n) -> p h j n", j=2)

        ident_made = sem("ident_made")
        w_loaded = sem("w_loaded")
        misc_loaded = sem("misc_loaded")
        setup_dve = sem("setup_dve")
        tanh_done = sem("tanh_done")
        setup_pe = sem("setup_pe")
        setup_copied = sem("setup_copied")
        x_loaded = [sem(f"x_loaded{s}") for s in range(U)]
        c_loaded = [sem(f"c_loaded{s}") for s in range(U)]
        bn1_done = sem("bn1_done")
        bn2_done = sem("bn2_done")
        bn3_done = sem("bn3_done")
        stats_a = sem("stats_a")
        stats_b = sem("stats_b")
        ln_a = sem("ln_a")
        ln_b = sem("ln_b")
        rs_a = sem("rs_a")
        rs_b = sem("rs_b")
        newton_a = sem("newton_a")
        newton_b = sem("newton_b")
        norm_a = sem("norm_a")
        norm_b = sem("norm_b")
        xn1_ready = sem("xn1_ready")
        xn1_turned = sem("xn1_turned")
        xn1T_ready = sem("xn1T_ready")
        h_done = sem("h_done")
        y_ready = sem("y_ready")
        o_done = sem("o_done")
        x1_ready = sem("x1_ready")
        masked_ready = sem("masked_ready")
        den_ready = sem("den_ready")
        masked_turned = sem("masked_turned")
        maskedT_ready = sem("maskedT_ready")
        mapped_done = sem("mapped_done")
        mapped_ready = sem("mapped_ready")
        xn2_scaled = sem("xn2_scaled")
        xn2_ready = sem("xn2_ready")
        xn2_turned = sem("xn2_turned")
        xn2T_ready = sem("xn2T_ready")
        scores_done = sem("scores_done")
        max_ready = sem("max_ready")
        probs_ready = sem("probs_ready")
        probs_turned = sem("probs_turned")
        probsT_ready = sem("probsT_ready")
        att_done = sem("att_done")
        inv_ready = sem("inv_ready")
        att_scaled = sem("att_scaled")
        att_ready = sem("att_ready")
        x2_ready = sem("x2_ready")
        xn3_ready = sem("xn3_ready")
        xn3_turned = sem("xn3_turned")
        xn3T_ready = sem("xn3T_ready")
        xn3_kept = [sem(f"xn3_kept{s}") for s in range(U)]
        g_done = sem("g_done")
        gate_ready = sem("gate_ready")
        score_ready = sem("score_ready")
        score_turned = sem("score_turned")
        rank_step = sem("rank_step")
        dropped_turned = sem("dropped_turned")
        drop_ready = sem("drop_ready")
        gelu_ready = sem("gelu_ready")
        picked = sem("picked")
        summed = sem("summed")
        stored = sem("stored")

        class Step:
            def __init__(self, kk, i):
                self.kk, self.i = kk, i
                self.looped = not isinstance(i, int)

            def has(self, lag):
                return self.looped or 0 <= self.kk - lag < NG

            def slot(self, lag):
                return (self.kk - lag) % U

            def group(self, lag):
                return self.kk - lag + U * self.i

            def upto(self, lag, each=1):
                return each * (self.kk - lag + 1) + (each * U) * self.i

            def landed(self, lag):
                return 16 * ((self.kk - lag) // U + 1) + 16 * self.i

        def run(engine, step):
            for kk in range(FIRST, LOOP0):
                step(Step(kk, 0))
            with engine.Fori(0, (LOOP1 - LOOP0) // U) as i:
                for kk in range(LOOP0, LOOP0 + U):
                    step(Step(kk, i))
            for kk in range(LOOP1, LAST + 1):
                step(Step(kk, 0))

        def reusable(eng, s, lag, signal):
            if s.looped or s.kk - lag >= U:
                eng.wait_ge(signal, s.upto(lag + U))

        def apart(eng, s):
            if s.looped:
                eng.nop(nofuse=True)

        def one_ago(eng, s, lag, signal):
            if s.looped or s.kk - lag >= 1:
                eng.wait_ge(signal, s.upto(lag + 1))

        TURNS = [(2, probs_turned, probsT_ready), (1, xn2_turned, xn2T_ready), (3, xn3_turned, xn3T_ready),
                 (-1, xn1_turned, xn1T_ready), (-1, masked_turned, maskedT_ready)]

        def turn_bank(s, n):
            return tr[(len(TURNS) * s.kk + n) % 2]

        def turn_free(eng, s, n):
            at = len(TURNS) * s.kk + n - 2
            while at >= len(TURNS) * FIRST:
                kk, m = divmod(at, len(TURNS))
                lag, _, copied = TURNS[m]
                if s.looped or 0 <= kk - lag < NG:
                    eng.wait_ge(copied, Step(kk, s.i).upto(lag))
                    return
                at -= 2

        block = stack.enter_context(nc.Block())

        @block.sync
        def _(sp):
            for n, w in enumerate((w_in, w_out, map_W)):
                sp.dma_start(w_nat[:, n, :], w).then_inc(w_loaded, 16)
            sp.dma_start(block_in[:, 0:D], w_block).then_inc(w_loaded, 16)
            sp.dma_start(cols[:, 0:1], a.rearrange("(d o) -> d o", o=1)).then_inc(misc_loaded, 16)
            sp.dma_start(cols[:, 1:2], b.rearrange("(d o) -> d o", o=1)).then_inc(misc_loaded, 16)
            sp.dma_start(block_in[:, D:D + 1], w_router.rearrange("(d o) -> d o", o=1)).then_inc(misc_loaded, 16)
            sp.dma_start(mask_int[:], mask).then_inc(misc_loaded, 16)
            sp.dma_start(mapb_all[:], map_b.rearrange("(o d) -> o d", o=1).broadcast_to([P, D])).then_inc(misc_loaded, 16)
            for part in range(3):
                for n, v in enumerate((b_in, b, b_out)):
                    sp.dma_start(bias_row[32 * part:32 * part + 1, n, :],
                                 v.rearrange("(o d) -> o d", o=1)).then_inc(misc_loaded, 16)

            def load(s, lag):
                if s.has(lag):
                    g = s.group(lag)
                    reusable(sp, s, lag, x1_ready)
                    sp.dma_start(x_in[:, s.slot(lag)], x_dram[g]).then_inc(x_loaded[s.slot(lag)], 16)
                    reusable(sp, s, lag, masked_ready)
                    sp.dma_start(c_in[:, s.slot(lag)], ctx_dram[g]).then_inc(c_loaded[s.slot(lag)], 16)

            def step(s):
                load(s, -1)
                if s.has(4):
                    g = s.group(4)
                    sp.wait_ge(xn3_ready, s.upto(4))
                    sp.dma_start(xn3_all[:, g], xn3[:, s.slot(4)]).then_inc(xn3_kept[s.slot(4)], 16)

            run(sp, step)
            for n in range(NG // 2):
                sp.wait_ge(summed, n + 1)
                sp.dma_start(out_dram[n], gate[:, 2 * n:2 * n + 2, :, 0:D]).then_inc(stored, 16)
            sp.wait_ge(stored, 16 * (NG // 2))

        @block.gpsimd
        def _(pool):
            nc.gpsimd.memset(ident[:], 0.0).then_inc(ident_made, 1)
            nc.gpsimd.memset(flip[:], 0.0).then_inc(ident_made, 1)
            pool.wait_ge(ident_made, 2)
            nc.gpsimd.affine_select(out=ident[:], in_=ident[:], compare_op=ALU.not_equal, fill=1.0, base=0,
                                    pattern=[[-1, P]], channel_multiplier=1).then_inc(ident_made, 1)
            nc.gpsimd.affine_select(out=flip[:], in_=flip[:], compare_op=ALU.not_equal, fill=1.0, base=1 - P,
                                    pattern=[[1, P]], channel_multiplier=1).then_inc(ident_made, 1)

            def norm2(s, lag):
                g, p = s.group(lag), s.slot(lag)
                pool.wait_ge(norm_b, s.upto(lag))
                reusable(pool, s, lag, xn2_turned)
                nc.gpsimd.tensor_tensor(xn2[:, p], xs[:, g], rb[:, p, :].unsqueeze(2).broadcast_to([P, J, D]),
                                        ALU.mult).then_inc(xn2_scaled, 1)
                pool.wait_ge(xn2_scaled, s.upto(lag))
                nc.gpsimd.tensor_tensor(xn2[:, p], xn2[:, p], nb[:, p, :].unsqueeze(2).broadcast_to([P, J, D]),
                                        ALU.add).then_inc(xn2_ready, 1)

            def mask_context(s, lag):
                g, p = s.group(lag), s.slot(lag)
                mask_cols = maskT[:].rearrange("q (g j) -> q g j", j=J)[:, g]
                pool.wait_ge(c_loaded[p], s.landed(lag))
                reusable(pool, s, lag, masked_turned)
                nc.gpsimd.tensor_tensor(c_masked[:, p], c_in[:, p], mask_cols.unsqueeze(2).broadcast_to([Q, J, D]),
                                        ALU.mult).then_inc(masked_ready, 1)

            def sum_column(s, lag):
                tiny_cols = mask_tiny[:].rearrange("q (g j) -> q g j", j=J)[:, s.group(lag)]
                reusable(pool, s, lag, att_done)
                nc.gpsimd.tensor_copy(c_mapped[:, s.slot(lag), :, D], tiny_cols).then_inc(den_ready, 1)

            def norm1(s, lag):
                p = s.slot(lag)
                q = s.kk % U
                pool.wait_ge(norm_a, s.kk - FIRST + 1 + U * s.i)
                reusable(pool, s, lag, xn1_turned)
                apart(pool, s)
                for j in range(J):
                    last = nc.gpsimd.tensor_scalar(xn1[:, p, j], x_in[:, p, j], ra[:, q, j:j + 1], na[:, q, j:j + 1],
                                                   ALU.mult, ALU.add)
                last.then_inc(xn1_ready, 1)

            def add_map_b(s, lag):
                p = s.slot(lag)
                pool.wait_ge(att_scaled, s.upto(lag))
                nc.gpsimd.tensor_tensor(att[:, p], att[:, p], mapb_all[:].unsqueeze(1).broadcast_to([P, J, D]),
                                        ALU.add).then_inc(att_ready, 1)

            def step(s):
                if s.has(1):
                    norm2(s, 1)
                if s.has(-1):
                    mask_context(s, -1)
                    norm1(s, -1)
                if s.has(2):
                    add_map_b(s, 2)
                if s.has(0):
                    sum_column(s, 0)

            pool.wait_ge(misc_loaded, 16 * 14)
            pool.wait_ge(setup_copied, 5)
            run(pool, step)
            for n in range(NG // 2):
                pool.wait_ge(picked, n + 1)
                nc.gpsimd.tensor_tensor(gate[:, 2 * n:2 * n + 2, :, 0:D].rearrange("p g j d -> p (g j) d"),
                                        gate[:, 2 * n:2 * n + 2, :, 0:D].rearrange("p g j d -> p (g j) d"),
                                        xs[:, 2 * n:2 * n + 2].rearrange("p g j d -> p (g j) d"), ALU.add).then_inc(summed, 1)

        @block.scalar
        def _(act):
            act.wait_ge(misc_loaded, 16 * 14)
            nc.scalar.activation(decay[:, 0:1], cols[:, 0:1], ACT.Tanh, scale=0.5).then_inc(tanh_done, 1)
            act.wait_ge(setup_dve, 2)
            nc.scalar.preload_act_table_set("natural_log_exp_and_others")

            def first_guess(s, mv, ln, y, stats, ln_sem, rs_sem, count, lo, hi, p):
                act.wait_ge(stats, count)
                nc.scalar.activation(ln[:, p, lo:hi], mv[:, p, lo:hi, 1], ACT.Ln, bias=eps_col[:, 0:1]).then_inc(ln_sem, 1)
                act.wait_ge(ln_sem, count)
                nc.scalar.activation(y[:, p, lo:hi], ln[:, p, lo:hi], ACT.Exp, scale=-0.5).then_inc(rs_sem, 1)

            def copy_turned(s, n, dst):
                lag, turned, copied = TURNS[n]
                rows, used = {0: (Q, att_done), 1: (P, scores_done), 2: (P, g_done), 3: (P, h_done),
                              4: (P, scores_done)}[n]
                width = J * Q if n == 4 else J * S
                act.wait_ge(turned, s.upto(lag))
                reusable(act, s, lag, used)
                if n == 4:
                    reusable(act, s, lag, mapped_done)
                nc.scalar.activation(dst[:, s.slot(lag)].rearrange("p j t -> p (j t)"),
                                     turn_bank(s, n)[0:rows, 0:width], ACT.Copy).then_inc(copied, 1)

            def exponentials(s, lag):
                p = s.slot(lag)
                act.wait_ge(max_ready, s.upto(lag))
                reusable(act, s, lag, probs_turned)
                for j in range(J):
                    last = nc.scalar.activation(probs[:, p, j], s_view[:, j], ACT.Exp, bias=negmax[:, p, j:j + 1])
                last.then_inc(probs_ready, 1)

            def step(s):
                if s.has(2):
                    exponentials(s, 2)
                if s.has(4):
                    act.wait_ge(g_done, s.upto(4))
                    nc.scalar.activation(gate[:, s.group(4)].rearrange("p (h j) n -> p h j n", h=2), wide_view,
                                         ACT.Copy).then_inc(gate_ready, 1)
                if s.has(2):
                    copy_turned(s, 0, probsT)
                if s.has(-1) or s.has(3):
                    lo, hi = (0 if s.has(-1) else J), (2 * J if s.has(3) else J)
                    first_guess(s, mva, lna, ya, stats_a, ln_a, rs_a, s.kk - FIRST + 1 + U * s.i, lo, hi, s.kk % U)
                if s.has(1):
                    copy_turned(s, 1, xn2T)
                if s.has(0):
                    act.wait_ge(mapped_done, s.upto(0))
                    reusable(act, s, 0, att_done)
                    nc.scalar.activation(c_mapped[:, s.slot(0), :, 0:D], m_ps[0:Q], ACT.Copy).then_inc(mapped_ready, 1)
                if s.has(3):
                    p, q, g = s.slot(3), s.kk % U, s.group(3)
                    act.wait_ge(norm_a, s.kk - FIRST + 1 + U * s.i)
                    reusable(act, s, 3, xn3_turned)
                    if s.looped or s.kk - 3 >= U:
                        act.wait_ge(xn3_kept[p], s.landed(3 + U))
                    for j in range(J):
                        last = nc.scalar.activation(xn3[:, p, j], xs[:, g, j], ACT.Identity, bias=na[:, q, J + j:J + j + 1],
                                                    scale=ra[:, q, J + j:J + j + 1])
                    last.then_inc(xn3_ready, 1)
                    copy_turned(s, 2, xn3T)
                if s.has(-1):
                    copy_turned(s, 3, xn1T)
                    copy_turned(s, 4, c_maskedT)
                if s.has(0):
                    first_guess(s, mvb, lnb, yb, stats_b, ln_b, rs_b, s.upto(0), 0, J, s.slot(0))

            run(act, step)
            act.wait_ge(gate_ready, NG)
            for n in range(NG // 2):
                v = gate[:, 2 * n:2 * n + 2, :, 0:D].rearrange("p g j d -> p (g j) d")
                nc.scalar.activation(v, v, ACT.Gelu_apprx_tanh).then_inc(gelu_ready, 1)

        @block.vector
        def _(dve):
            made = [0]

            def made_then_wait(ins):
                made[0] += 1
                ins.then_inc(setup_dve, 1)
                dve.wait_ge(setup_dve, made[0])

            nc.vector.memset(ones_bf[:], 1.0)
            made_then_wait(nc.vector.memset(bias_parts[:], 0.0))
            made_then_wait(nc.vector.memset(eps_col[:], EPS))
            nc.vector.memset(bout_parts[:], 0.0)
            made_then_wait(nc.vector.memset(decay_row[:], 1.0))
            dve.wait_ge(misc_loaded, 16 * 14)
            dve.wait_ge(w_loaded, 16 * 4)
            nc.vector.tensor_scalar(w_nat[:, 0], w_nat[:, 0], cols[:, 1:2], None, ALU.mult)
            made_then_wait(nc.vector.tensor_copy(mask_nat[:], mask_int[:]))
            dve.wait_ge(tanh_done, 1)
            made_then_wait(nc.vector.tensor_scalar(decay[:, 1:2], decay[:, 0:1], 0.5, 0.5, ALU.mult, ALU.add))
            made_then_wait(nc.vector.tensor_scalar(decay_row[:], decay_row[:], decay[:, 1:2], None, ALU.mult))
            nc.vector.memset(decay_row[:, :, 0], 0.0)
            for r in (0, 32, 64):
                row = slice(r, r + 1)
                made_then_wait(nc.vector.tensor_tensor(bias_row[row, 1], bias_row[row, 0], bias_row[row, 1], ALU.mult))
                v = bias_row[row, 1:3]
                made_then_wait(nc.vector.tensor_copy(bias_hi[row], v))
                if r:
                    made_then_wait(nc.vector.tensor_tensor(bias_rest[row], v, bias_hi[row], ALU.subtract))
                    made_then_wait(nc.vector.tensor_copy(bias_mid[row], bias_rest[row]))
                if r == 64:
                    made_then_wait(nc.vector.tensor_tensor(bias_rest[row], bias_rest[row], bias_mid[row], ALU.subtract))
                src = {0: bias_hi, 32: bias_mid, 64: bias_rest}[r]
                nc.vector.tensor_copy(bias_parts[row, 0], src[row, 0])
                made_then_wait(nc.vector.tensor_copy(bout_parts[row], src[row, 1].unsqueeze(1).broadcast_to([1, J, P])))
            for n, dst in enumerate((w_inT, w_outT, mapWT)):
                dve.wait_ge(setup_pe, n + 1)
                nc.vector.tensor_copy(dst[:, 0:P], tr[n % 2][:, 0:P]).then_inc(setup_copied, 1)
            dve.wait_ge(setup_pe, 4)
            nc.vector.tensor_copy(maskT[:], tr[1][0:Q, 0:B]).then_inc(setup_copied, 1)
            nc.vector.tensor_scalar(mask_tiny[:], tr[1][0:Q, 0:B], TINY, None, ALU.add).then_inc(setup_copied, 1)

            def newton(mv, y, t, r, n, p, lo, hi, chain, count, done):
                var, mean = mv[:, p, lo:hi, 1], mv[:, p, lo:hi, 0]
                y, t0, t1, r, n = y[:, p, lo:hi], t[:, p, 0, lo:hi], t[:, p, 1, lo:hi], r[:, p, lo:hi], n[:, p, lo:hi]
                nc.vector.scalar_tensor_tensor(t0, y, -0.5, y, ALU.mult, ALU.mult).then_inc(chain, 1)
                dve.wait_ge(chain, count + 1)
                nc.vector.scalar_tensor_tensor(t1, var, EPS, t0, ALU.add, ALU.mult).then_inc(chain, 1)
                dve.wait_ge(chain, count + 2)
                nc.vector.scalar_tensor_tensor(r, t1, 1.5, y, ALU.add, ALU.mult).then_inc(chain, 1)
                dve.wait_ge(chain, count + 3)
                nc.vector.scalar_tensor_tensor(n, mean, -1.0, r, ALU.mult, ALU.mult).then_inc(done, 1)

            def statistics(s, lag, src, bn, mv, col0, p, bn_sem, agg_sem):
                q = s.slot(lag)
                apart(dve, s)
                for j in range(J):
                    last = nc.vector.bn_stats(bn[:, q, j], src[:, j])
                last.then_inc(bn_sem, 1)
                dve.wait_ge(bn_sem, s.upto(lag))
                apart(dve, s)
                for j in range(J):
                    last = nc.vector.bn_aggr(mv[:, p, col0 + j], bn[:, q, j])
                if agg_sem is not None:
                    last.then_inc(agg_sem, 1)

            def step(s):
                nth = s.kk - FIRST + U * s.i
                if s.has(1):
                    dve.wait_ge(rs_b, s.upto(1))
                    newton(mvb, yb, tb, rb, nb, s.slot(1), 0, J, newton_b, s.upto(2, 3), norm_b)
                if s.has(2):
                    dve.wait_ge(scores_done, s.upto(2))
                    reusable(dve, s, 2, probs_ready)
                    nc.vector.tensor_reduce(negmax[:, s.slot(2)], s_view, AX_X, ALU.max, negate=True).then_inc(max_ready, 1)
                if s.has(3):
                    g = s.group(3)
                    dve.wait_ge(att_ready, s.upto(3))
                    nc.vector.scalar_tensor_tensor(xs[:, g].rearrange("p j d -> p (j d)"),
                                                   att[:, s.slot(3)].rearrange("p j d -> p (j d)"), 0.0,
                                                   xs[:, g].rearrange("p j d -> p (j d)"), ALU.max,
                                                   ALU.add).then_inc(x2_ready, 1)
                a_last = s.has(3)
                if s.has(-1):
                    dve.wait_ge(x_loaded[s.slot(-1)], s.landed(-1))
                    statistics(s, -1, x_in[:, s.slot(-1)], bn1, mva, 0, s.kk % U, bn1_done, None if a_last else stats_a)
                if s.has(3):
                    dve.wait_ge(x2_ready, s.upto(3))
                    statistics(s, 3, xs[:, s.group(3)], bn3, mva, J, s.kk % U, bn3_done, stats_a)
                if s.has(0):
                    dve.wait_ge(h_done, s.upto(0))
                    reusable(dve, s, 0, o_done)
                    nc.vector.tensor_tensor_scan(yT[:, s.slot(0)].rearrange("p j t -> p (j t)"),
                                                 decay_row[:].rearrange("p j t -> p (j t)"),
                                                 h_ps[:].rearrange("p j t -> p (j t)"), 0.0, ALU.mult,
                                                 ALU.add).then_inc(y_ready, 1)
                if s.has(-1) or s.has(3):
                    lo, hi = (0 if s.has(-1) else J), (2 * J if s.has(3) else J)
                    dve.wait_ge(rs_a, nth + 1)
                    newton(mva, ya, ta, ra, na, s.kk % U, lo, hi, newton_a, 3 * nth, norm_a)
                if s.has(2):
                    p = s.slot(2)
                    dve.wait_ge(att_done, s.upto(2))
                    nc.vector.reciprocal(inv[:, p].rearrange("p (h j) -> p h j", h=2),
                                         wide_view[:, :, :, D]).then_inc(inv_ready, 1)
                    dve.wait_ge(inv_ready, s.upto(2))
                    nc.vector.tensor_tensor(att[:, p].rearrange("p (h j) d -> p h j d", h=2), wide_view[:, :, :, 0:D],
                                            inv[:, p].rearrange("p (h j) -> p h j", h=2).unsqueeze(3)
                                            .broadcast_to([P, 2, 2, D]), ALU.mult).then_inc(att_scaled, 1)
                if s.has(0):
                    g = s.group(0)
                    dve.wait_ge(o_done, s.upto(0))
                    nc.vector.tensor_tensor(xs[:, g], o_ps[:], x_in[:, s.slot(0)], ALU.add).then_inc(x1_ready, 1)
                    dve.wait_ge(x1_ready, s.upto(0))
                    statistics(s, 0, xs[:, g], bn2, mvb, 0, s.slot(0), bn2_done, stats_b)

            run(dve, step)

            dve.wait_ge(gate_ready, NG)
            nc.vector.tensor_copy(score[:].rearrange("p (g j) -> p g j", j=J), gate[:, :, :, D]).then_inc(score_ready, 1)
            dve.wait_ge(score_turned, 1)
            ranks = [0]

            def ranked_then_wait(ins):
                ranks[0] += 1
                ins.then_inc(rank_step, 1)
                dve.wait_ge(rank_step, ranks[0])

            ranked_then_wait(nc.vector.tensor_scalar(ranked[:], tr[0][0:B, 0:S], -1.0, None, ALU.mult))
            for _ in range(ROUNDS):
                ranked_then_wait(nc.vector.max(top8[:], ranked[:]))
                ranked_then_wait(nc.vector.match_replace(ranked[:], top8[:], ranked[:], LOWEST))
            ranked_then_wait(nc.vector.tensor_scalar(dropped[:, ::-1], ranked[:], LOWEST, None, ALU.is_equal))
            dve.wait_ge(dropped_turned, 1)
            ranked_then_wait(nc.vector.tensor_copy(droppedT[:], tr[1][:, 0:B]))
            for n in range(NG // 2):
                dve.wait_ge(gelu_ready, n + 1)
                if n == 0:
                    for q in range(U):
                        dve.wait_ge(xn3_kept[q], 16 * (NG // U))
                b0 = 2 * J * n
                nc.vector.copy_predicated(gate[:, 2 * n:2 * n + 2, :, 0:D].rearrange("p g j d -> p (g j) d"),
                                          droppedT[:, b0:b0 + 2 * J].bitcast(mybir.dt.uint32).unsqueeze(2)
                                          .broadcast_to([P, 2 * J, D]),
                                          xn3_all[:, 2 * n:2 * n + 2].rearrange("p g j d -> p (g j) d")).then_inc(picked, 1)

        @block.tensor
        def _(pe):
            pe.wait_ge(ident_made, 4)
            pe.wait_ge(setup_dve, 4)
            pe.wait_ge(w_loaded, 16 * 4)
            for n in range(3):
                if n >= 2:
                    pe.wait_ge(setup_copied, n - 1)
                nc.tensor.transpose(tr[n % 2][:, 0:P], w_nat[:, n], ident[:]).then_inc(setup_pe, 1)
            pe.wait_ge(setup_copied, 2)
            nc.tensor.transpose(tr[1][0:Q, 0:B], mask_nat[:], ident[0:B, 0:B]).then_inc(setup_pe, 1)
            pe.wait_ge(setup_copied, 5)

            def turn(s, n, src, ready, rows, cols_):
                lag, turned, _ = TURNS[n]
                pe.wait_ge(ready, s.upto(lag))
                turn_free(pe, s, n)
                dst = turn_bank(s, n)
                for j in range(J):
                    last = nc.tensor.transpose(dst[0:cols_, j * rows:(j + 1) * rows], src[0:rows, s.slot(lag), j],
                                               ident[0:rows, 0:rows])
                last.then_inc(turned, 1)

            def input_product(s, lag):
                pe.wait_ge(xn1T_ready, s.upto(lag))
                one_ago(pe, s, lag, y_ready)
                flat = h_ps[:].rearrange("p j t -> p (j t)")
                nc.tensor.matmul(flat, w_inT[:], xn1T[:, s.slot(lag)].rearrange("p j t -> p (j t)"), start=True, stop=False)
                nc.tensor.matmul(flat, bias_parts[:, 0], ones_bf[:], start=False, stop=True).then_inc(h_done, 1)

            def output_product(s, lag):
                pe.wait_ge(y_ready, s.upto(lag))
                one_ago(pe, s, lag, x1_ready)
                flat = o_ps[:].rearrange("p j t -> p (j t)")
                nc.tensor.matmul(flat, ones_bf[:, 0:S], bout_parts[:].rearrange("p j d -> p (j d)"), start=True, stop=False)
                for j in range(J):
                    last = nc.tensor.matmul(o_ps[:, j], yT[:, s.slot(lag), j], w_outT[:], start=False, stop=(j == J - 1))
                last.then_inc(o_done, 1)

            def map_context(s, lag):
                pe.wait_ge(maskedT_ready, s.upto(lag))
                one_ago(pe, s, lag, mapped_ready)
                for j in range(J):
                    last = nc.tensor.matmul(m_ps[0:Q, j], c_maskedT[:, s.slot(lag), j], mapWT[:], start=True, stop=True)
                last.then_inc(mapped_done, 1)

            def scores(s, lag):
                pe.wait_ge(xn2T_ready, s.upto(lag))
                one_ago(pe, s, lag, probs_ready)
                for j in range(J):
                    last = nc.tensor.matmul(s_view[:, j], xn2T[:, s.slot(lag), j], c_maskedT[:, s.slot(lag), j],
                                            start=True, stop=True)
                last.then_inc(scores_done, 1)

            def attend(s, lag):
                pe.wait_ge(probsT_ready, s.upto(lag))
                pe.wait_ge(mapped_ready, s.upto(lag))
                pe.wait_ge(den_ready, s.upto(lag))
                if s.has(lag + 2):
                    pe.wait_ge(gate_ready, s.upto(lag + 2))
                else:
                    one_ago(pe, s, lag, att_scaled)
                for j in range(J):
                    last = nc.tensor.matmul(wide_view[:, j // 2, j % 2], probsT[:, s.slot(lag), j],
                                            c_mapped[:, s.slot(lag), j], start=True, stop=True)
                last.then_inc(att_done, 1)

            def feed_forward(s, lag):
                pe.wait_ge(xn3T_ready, s.upto(lag))
                if s.has(lag - 1):
                    pe.wait_ge(att_scaled, s.upto(lag - 1))
                else:
                    one_ago(pe, s, lag, gate_ready)
                for j in range(J):
                    last = nc.tensor.matmul(wide_view[:, j // 2, j % 2], xn3T[:, s.slot(lag), j], block_in[:],
                                            start=True, stop=True)
                last.then_inc(g_done, 1)

            def step(s):
                if s.has(4):
                    feed_forward(s, 4)
                if s.has(0):
                    input_product(s, 0)
                if s.has(2):
                    turn(s, 0, probs, probs_ready, P, Q)
                if s.has(0):
                    map_context(s, 0)
                if s.has(2):
                    attend(s, 2)
                if s.has(1):
                    turn(s, 1, xn2, xn2_ready, P, D)
                if s.has(0):
                    output_product(s, 0)
                if s.has(1):
                    scores(s, 1)
                if s.has(3):
                    turn(s, 2, xn3, xn3_ready, P, D)
                if s.has(-1):
                    turn(s, 3, xn1, xn1_ready, P, D)
                    turn(s, 4, c_masked, masked_ready, Q, D)

            run(pe, step)
            pe.wait_ge(score_ready, 1)
            nc.tensor.transpose(tr[0][0:B, 0:S], score[:], flip[:]).then_inc(score_turned, 1)
            pe.wait_ge(rank_step, 2 * ROUNDS + 2)
            nc.tensor.transpose(tr[1][:, 0:B], dropped[:], ident[0:B, 0:B]).then_inc(dropped_turned, 1)


INPUTS = ["x", "ctx_1024", "mask_BxS2_ik0", "L0_attn_w_in", "L0_attn_b_in", "L0_attn_a", "L0_attn_b", "L0_attn_w_out",
          "L0_attn_b_out", "L0_xattn_map_W", "L0_xattn_map_b", "L0_ffn_w_router", "L0_ffn_w_block"]


def kernel(**inputs):
    import numpy as np
    import concourse.bacc as bacc
    from concourse.bass_utils import run_bass_kernel_spmd

    nc = bacc.Bacc("TRN2", target_bir_lowering=False, num_devices=1)
    arrays, args = {}, []
    for name in INPUTS:
        array = np.ascontiguousarray(inputs[name])
        arrays[f"in_{name}"] = array
        args.append(nc.dram_tensor(f"in_{name}", array.shape, mybir.dt.from_np(array.dtype), kind="ExternalInput").ap())
    out = nc.dram_tensor("out", inputs["x"].shape, F32, kind="ExternalOutput").ap()
    decoder_layer(nc, *args, out)
    result = run_bass_kernel_spmd(nc, [arrays], core_ids=[0])
    return result.results[0]["out"]
```

```python
from contextlib import ExitStack

import concourse.bass as bass
from concourse import mybir

F32 = mybir.dt.float32
BF16 = mybir.dt.bfloat16
I32 = mybir.dt.int32
ALU = mybir.AluOpType
ACT = mybir.ActivationFunctionType
AX_X = mybir.AxisListType.X

P = 128
J = 4
U = 2
EPS = 1e-5
TINY = 1e-13
LOWEST = -3.0e38
CAPACITY = 0.75


def decoder_layer(nc: bass.Bass, x, ctx, mask, w_in, b_in, a, b, w_out, b_out, map_W, map_b, w_router, w_block, out):
    B, S, D = x.shape
    Q = ctx.shape[1]
    NG = B // J
    DROP = S - max(1, int(S * CAPACITY))
    ROUNDS = DROP // 8
    assert S == P and D == P and B % (J * U) == 0 and DROP % 8 == 0
    FIRST, LAST = -1, NG + 2
    LOOP0, LOOP1 = 5, NG - 1
    assert (LOOP1 - LOOP0) % U == 0 and LOOP1 - LOOP0 > 0

    x_dram = x.rearrange("(g j) t d -> g t j d", j=J)
    ctx_dram = ctx.rearrange("(g j) q d -> g q j d", j=J)
    out_dram = out.rearrange("(g j) t d -> g t j d", j=2 * J)

    with ExitStack() as stack:
        def sb(name, shape, dt=F32):
            return stack.enter_context(nc.sbuf_tensor(name, shape, dt))

        def ps(name, shape):
            return stack.enter_context(nc.psum_tensor(name, shape, F32))

        def sem(name):
            return stack.enter_context(nc.semaphore(name))

        ident = sb("ident", [P, P])
        flip = sb("flip", [P, P])
        w_nat = sb("w_nat", [P, 3, P])
        w_inT = sb("w_inT", [P, P])
        w_outT = sb("w_outT", [P, P])
        mapWT = sb("mapWT", [P, P])
        block_in = sb("block_in", [P, P + 1])
        cols = sb("cols", [P, 2])
        decay = sb("decay", [P, 2])
        decay_row = sb("decay_row", [P, J, S])
        mapb_all = sb("mapb_all", [P, P])
        eps_col = sb("eps_col", [P, 1])
        mask_int = sb("mask_int", [B, Q], I32)
        mask_nat = sb("mask_nat", [B, Q])
        maskT = sb("maskT", [Q, B])
        mask_tiny = sb("mask_tiny", [Q, B])
        bias_row = sb("bias_row", [65, 3, P])
        bias_rest = sb("bias_rest", [65, 2, P])
        bias_hi = sb("bias_hi", [65, 2, P], BF16)
        bias_mid = sb("bias_mid", [65, 2, P], BF16)
        bias_parts = sb("bias_parts", [65, 2, P], BF16)
        bout_parts = sb("bout_parts", [65, J, P], BF16)
        ones_bf = sb("ones_bf", [65, J * S], BF16)

        x_in = sb("x_in", [P, U, J, D])
        c_in = sb("c_in", [Q, U, J, D])
        c_masked = sb("c_masked", [Q, U, J, D])
        c_maskedT = sb("c_maskedT", [P, U, J, Q])
        xn1 = sb("xn1", [P, U, J, D])
        xn1T = sb("xn1T", [P, U, J, S])
        yT = sb("yT", [P, U, J, S])
        xn2 = sb("xn2", [P, U, J, D])
        xn2T = sb("xn2T", [P, U, J, S])
        probs = sb("probs", [P, U, J, Q])
        probsT = sb("probsT", [Q, U, J, S])
        c_mapped = sb("c_mapped", [Q, U, J, D + 1])
        att = sb("att", [P, U, J, D])
        xn3 = sb("xn3", [P, U, J, D])
        xn3T = sb("xn3T", [P, U, J, S])
        bn1 = sb("bn1", [P, U, J, 6])
        bn2 = sb("bn2", [P, U, J, 6])
        bn3 = sb("bn3", [P, U, J, 6])
        mva = sb("mva", [P, U, J, 2])
        lna = sb("lna", [P, U, J])
        ya = sb("ya", [P, U, J])
        ta = sb("ta", [P, U, 2, J])
        ra = sb("ra", [P, U, J])
        na = sb("na", [P, U, J])
        mvb = sb("mvb", [P, U, 2 * J, 2])
        lnb = sb("lnb", [P, U, 2 * J])
        yb = sb("yb", [P, U, 2 * J])
        tb = sb("tb", [P, U, 2, 2 * J])
        rb = sb("rb", [P, U, 2 * J])
        nb = sb("nb", [P, U, 2 * J])
        negmax = sb("negmax", [P, U, J])
        inv = sb("inv", [P, U, J])

        xs = sb("xs", [P, NG, J, D])
        xn3_all = sb("xn3_all", [P, NG, J, D])
        gate = sb("gate", [P, NG, J, D + 1])
        score = sb("score", [P, B])
        ranked = sb("ranked", [B, S])
        top8 = sb("top8", [B, 8])
        dropped = sb("dropped", [B, S])
        droppedT = sb("droppedT", [P, B])

        tr = [ps("tr0", [P, 512]), ps("tr1", [P, 512])]
        h_ps = ps("h_ps", [P, J, S])
        o_ps = ps("o_ps", [P, J, D])
        s_ps = ps("s_ps", [P, 512])
        m_ps = ps("m_ps", [P, J, D])
        wide = ps("wide", [P, 2, 512])
        s_view = s_ps[:, 0:J * Q].rearrange("p (j q) -> p j q", j=J)
        wide_view = wide[:, :, 0:2 * (D + 1)].rearrange("p h (j n) -> p h j n", j=2)

        ident_made = sem("ident_made")
        w_loaded = sem("w_loaded")
        misc_loaded = sem("misc_loaded")
        setup_dve = sem("setup_dve")
        tanh_done = sem("tanh_done")
        setup_pe = sem("setup_pe")
        setup_copied = sem("setup_copied")
        x_loaded = [sem(f"x_loaded{s}") for s in range(U)]
        c_loaded = [sem(f"c_loaded{s}") for s in range(U)]
        bn1_done = sem("bn1_done")
        bn2_done = sem("bn2_done")
        bn3_done = sem("bn3_done")
        stats_a = sem("stats_a")
        stats_b = sem("stats_b")
        ln_a = sem("ln_a")
        ln_b = sem("ln_b")
        rs_a = sem("rs_a")
        rs_b = sem("rs_b")
        newton_a = sem("newton_a")
        newton_b = sem("newton_b")
        norm_a = sem("norm_a")
        norm_b = sem("norm_b")
        xn1_ready = sem("xn1_ready")
        xn1_turned = sem("xn1_turned")
        xn1T_ready = sem("xn1T_ready")
        h_done = sem("h_done")
        y_ready = sem("y_ready")
        o_done = sem("o_done")
        x1_ready = sem("x1_ready")
        masked_ready = sem("masked_ready")
        den_ready = sem("den_ready")
        masked_turned = sem("masked_turned")
        maskedT_ready = sem("maskedT_ready")
        mapped_done = sem("mapped_done")
        mapped_ready = sem("mapped_ready")
        xn2_scaled = sem("xn2_scaled")
        xn2_ready = sem("xn2_ready")
        xn2_turned = sem("xn2_turned")
        xn2T_ready = sem("xn2T_ready")
        scores_done = sem("scores_done")
        max_ready = sem("max_ready")
        probs_ready = sem("probs_ready")
        probs_turned = sem("probs_turned")
        probsT_ready = sem("probsT_ready")
        att_done = sem("att_done")
        inv_ready = sem("inv_ready")
        att_scaled = sem("att_scaled")
        att_ready = sem("att_ready")
        x2_ready = sem("x2_ready")
        xn3_ready = sem("xn3_ready")
        xn3_turned = sem("xn3_turned")
        xn3T_ready = sem("xn3T_ready")
        xn3_kept = [sem(f"xn3_kept{s}") for s in range(U)]
        g_done = sem("g_done")
        gate_ready = sem("gate_ready")
        score_ready = sem("score_ready")
        score_turned = sem("score_turned")
        rank_step = sem("rank_step")
        dropped_turned = sem("dropped_turned")
        drop_ready = sem("drop_ready")
        gelu_ready = sem("gelu_ready")
        picked = sem("picked")
        summed = sem("summed")
        stored = sem("stored")

        class Step:
            def __init__(self, kk, i):
                self.kk, self.i = kk, i
                self.looped = not isinstance(i, int)

            def has(self, lag):
                return self.looped or 0 <= self.kk - lag < NG

            def slot(self, lag):
                return (self.kk - lag) % U

            def group(self, lag):
                return self.kk - lag + U * self.i

            def upto(self, lag, each=1):
                return each * (self.kk - lag + 1) + (each * U) * self.i

            def landed(self, lag):
                return 16 * ((self.kk - lag) // U + 1) + 16 * self.i

        def run(engine, step):
            for kk in range(FIRST, LOOP0):
                step(Step(kk, 0))
            with engine.Fori(0, (LOOP1 - LOOP0) // U) as i:
                for kk in range(LOOP0, LOOP0 + U):
                    step(Step(kk, i))
            for kk in range(LOOP1, LAST + 1):
                step(Step(kk, 0))

        def reusable(eng, s, lag, signal):
            if s.looped or s.kk - lag >= U:
                eng.wait_ge(signal, s.upto(lag + U))

        def apart(eng, s):
            if s.looped:
                eng.nop(nofuse=True)

        def one_ago(eng, s, lag, signal):
            if s.looped or s.kk - lag >= 1:
                eng.wait_ge(signal, s.upto(lag + 1))

        TURNS = [(3, xn3_turned, xn3T_ready),
                 (1, xn2_turned, xn2T_ready),
                 (-1, xn1_turned, xn1T_ready),
                 (1, probs_turned, probsT_ready),
                 (-1, masked_turned, maskedT_ready)]
        TURN_OF = {turned: n for n, (_, turned, _) in enumerate(TURNS)}

        def turn_bank(s, turned):
            return tr[(len(TURNS) * s.kk + TURN_OF[turned]) % 2]

        def turn_free(eng, s, turned):
            at = len(TURNS) * s.kk + TURN_OF[turned] - 2
            while at >= len(TURNS) * FIRST:
                kk, m = divmod(at, len(TURNS))
                lag, _, copied = TURNS[m]
                if s.looped or 0 <= kk - lag < NG:
                    eng.wait_ge(copied, Step(kk, s.i).upto(lag))
                    return
                at -= 2

        block = stack.enter_context(nc.Block())

        @block.sync
        def _(sp):
            for n, w in enumerate((w_in, w_out, map_W)):
                sp.dma_start(w_nat[:, n, :], w).then_inc(w_loaded, 16)
            sp.dma_start(block_in[:, 0:D], w_block).then_inc(w_loaded, 16)
            sp.dma_start(cols[:, 0:1], a.rearrange("(d o) -> d o", o=1)).then_inc(misc_loaded, 16)
            sp.dma_start(cols[:, 1:2], b.rearrange("(d o) -> d o", o=1)).then_inc(misc_loaded, 16)
            sp.dma_start(block_in[:, D:D + 1], w_router.rearrange("(d o) -> d o", o=1)).then_inc(misc_loaded, 16)
            sp.dma_start(mask_int[:], mask).then_inc(misc_loaded, 16)
            sp.dma_start(mapb_all[:], map_b.rearrange("(o d) -> o d", o=1).broadcast_to([P, D])).then_inc(misc_loaded, 16)
            for part in range(3):
                for n, v in enumerate((b_in, b, b_out)):
                    sp.dma_start(bias_row[32 * part:32 * part + 1, n, :],
                                 v.rearrange("(o d) -> o d", o=1)).then_inc(misc_loaded, 16)

            def load(s, lag):
                if s.has(lag):
                    g = s.group(lag)
                    reusable(sp, s, lag, x1_ready)
                    sp.dma_start(x_in[:, s.slot(lag)], x_dram[g]).then_inc(x_loaded[s.slot(lag)], 16)
                    reusable(sp, s, lag, masked_ready)
                    sp.dma_start(c_in[:, s.slot(lag)], ctx_dram[g]).then_inc(c_loaded[s.slot(lag)], 16)

            def step(s):
                load(s, -1)
                if s.has(3):
                    g = s.group(3)
                    sp.wait_ge(xn3_ready, s.upto(3))
                    sp.dma_start(xn3_all[:, g], xn3[:, s.slot(3)]).then_inc(xn3_kept[s.slot(3)], 16)

            run(sp, step)
            for n in range(NG // 2):
                sp.wait_ge(summed, n + 1)
                sp.dma_start(out_dram[n], gate[:, 2 * n:2 * n + 2, :, 0:D]).then_inc(stored, 16)
            sp.wait_ge(stored, 16 * (NG // 2))

        @block.gpsimd
        def _(pool):
            nc.gpsimd.memset(ident[:], 0.0).then_inc(ident_made, 1)
            nc.gpsimd.memset(flip[:], 0.0).then_inc(ident_made, 1)
            pool.wait_ge(ident_made, 2)
            nc.gpsimd.affine_select(out=ident[:], in_=ident[:], compare_op=ALU.not_equal, fill=1.0, base=0,
                                    pattern=[[-1, P]], channel_multiplier=1).then_inc(ident_made, 1)
            nc.gpsimd.affine_select(out=flip[:], in_=flip[:], compare_op=ALU.not_equal, fill=1.0, base=1 - P,
                                    pattern=[[1, P]], channel_multiplier=1).then_inc(ident_made, 1)

            def norm2(s, lag):
                if not s.has(lag):
                    return
                g, p = s.group(lag), s.slot(lag)
                pool.wait_ge(norm_b, s.upto(lag))
                reusable(pool, s, lag, xn2_turned)
                nc.gpsimd.tensor_tensor(xn2[:, p], xs[:, g], rb[:, p, 0:J].unsqueeze(2).broadcast_to([P, J, D]),
                                        ALU.mult).then_inc(xn2_scaled, 1)
                pool.wait_ge(xn2_scaled, s.upto(lag))
                nc.gpsimd.tensor_tensor(xn2[:, p], xn2[:, p], nb[:, p, 0:J].unsqueeze(2).broadcast_to([P, J, D]),
                                        ALU.add).then_inc(xn2_ready, 1)

            def mask_context(s, lag):
                if not s.has(lag):
                    return
                g, p = s.group(lag), s.slot(lag)
                mask_cols = maskT[:].rearrange("q (g j) -> q g j", j=J)[:, g]
                pool.wait_ge(c_loaded[p], s.landed(lag))
                reusable(pool, s, lag, masked_turned)
                nc.gpsimd.tensor_tensor(c_masked[:, p], c_in[:, p], mask_cols.unsqueeze(2).broadcast_to([Q, J, D]),
                                        ALU.mult).then_inc(masked_ready, 1)

            def sum_column(s, lag):
                if not s.has(lag):
                    return
                tiny_cols = mask_tiny[:].rearrange("q (g j) -> q g j", j=J)[:, s.group(lag)]
                reusable(pool, s, lag, att_done)
                nc.gpsimd.tensor_copy(c_mapped[:, s.slot(lag), :, D], tiny_cols).then_inc(den_ready, 1)

            def norm1(s, lag):
                if not s.has(lag):
                    return
                p = s.slot(lag)
                pool.wait_ge(norm_a, s.upto(lag))
                reusable(pool, s, lag, xn1_turned)
                apart(pool, s)
                for j in range(J):
                    last = nc.gpsimd.tensor_scalar(xn1[:, p, j], x_in[:, p, j], ra[:, p, j:j + 1], na[:, p, j:j + 1],
                                                   ALU.mult, ALU.add)
                last.then_inc(xn1_ready, 1)

            def add_map_b(s, lag):
                if not s.has(lag):
                    return
                p = s.slot(lag)
                pool.wait_ge(att_scaled, s.upto(lag))
                nc.gpsimd.tensor_tensor(att[:, p], att[:, p], mapb_all[:].unsqueeze(1).broadcast_to([P, J, D]),
                                        ALU.add).then_inc(att_ready, 1)

            def step(s):
                norm2(s, 1)
                add_map_b(s, 2)
                norm1(s, -1)
                sum_column(s, 0)
                mask_context(s, -1)

            pool.wait_ge(misc_loaded, 16 * 14)
            pool.wait_ge(setup_copied, 5)
            run(pool, step)
            for n in range(NG // 2):
                pool.wait_ge(picked, n + 1)
                nc.gpsimd.tensor_tensor(gate[:, 2 * n:2 * n + 2, :, 0:D].rearrange("p g j d -> p (g j) d"),
                                        gate[:, 2 * n:2 * n + 2, :, 0:D].rearrange("p g j d -> p (g j) d"),
                                        xs[:, 2 * n:2 * n + 2].rearrange("p g j d -> p (g j) d"), ALU.add).then_inc(summed, 1)

        @block.scalar
        def _(act):
            act.wait_ge(misc_loaded, 16 * 14)
            nc.scalar.activation(decay[:, 0:1], cols[:, 0:1], ACT.Tanh, scale=0.5).then_inc(tanh_done, 1)
            act.wait_ge(setup_dve, 2)
            nc.scalar.preload_act_table_set("natural_log_exp_and_others")

            def first_guess(s, mv, ln, y, stats, ln_sem, rs_sem, count, lo, hi, p):
                act.wait_ge(stats, count)
                nc.scalar.activation(ln[:, p, lo:hi], mv[:, p, lo:hi, 1], ACT.Ln, bias=eps_col[:, 0:1]).then_inc(ln_sem, 1)
                act.wait_ge(ln_sem, count)
                nc.scalar.activation(y[:, p, lo:hi], ln[:, p, lo:hi], ACT.Exp, scale=-0.5).then_inc(rs_sem, 1)

            def guess_a(s, lag):
                if s.has(lag):
                    first_guess(s, mva, lna, ya, stats_a, ln_a, rs_a, s.upto(lag), 0, J, s.slot(lag))

            def guess_b(s):
                if s.has(0) or s.has(2):
                    lo, hi = (0 if s.has(0) else J), (2 * J if s.has(2) else J)
                    first_guess(s, mvb, lnb, yb, stats_b, ln_b, rs_b, s.upto(0), lo, hi, s.slot(0))

            def copy_turned(s, turned, dst, rows, width, *used):
                lag, _, copied = TURNS[TURN_OF[turned]]
                if not s.has(lag):
                    return
                act.wait_ge(turned, s.upto(lag))
                for signal in used:
                    reusable(act, s, lag, signal)
                nc.scalar.activation(dst[:, s.slot(lag)].rearrange("p j t -> p (j t)"),
                                     turn_bank(s, turned)[0:rows, 0:width], ACT.Copy).then_inc(copied, 1)

            def exponentials(s, lag):
                if not s.has(lag):
                    return
                p = s.slot(lag)
                act.wait_ge(max_ready, s.upto(lag))
                reusable(act, s, lag, probs_turned)
                for j in range(J):
                    last = nc.scalar.activation(probs[:, p, j], s_view[:, j], ACT.Exp, bias=negmax[:, p, j:j + 1])
                last.then_inc(probs_ready, 1)

            def copy_gate(s, lag):
                if not s.has(lag):
                    return
                act.wait_ge(g_done, s.upto(lag))
                nc.scalar.activation(gate[:, s.group(lag)].rearrange("p (h j) n -> p h j n", h=2), wide_view,
                                     ACT.Copy).then_inc(gate_ready, 1)

            def copy_mapped(s, lag):
                if not s.has(lag):
                    return
                act.wait_ge(mapped_done, s.upto(lag))
                reusable(act, s, lag, att_done)
                nc.scalar.activation(c_mapped[:, s.slot(lag), :, 0:D], m_ps[0:Q], ACT.Copy).then_inc(mapped_ready, 1)

            def norm3(s, lag):
                if not s.has(lag):
                    return
                p, q, g = s.slot(lag), s.slot(1), s.group(lag)
                act.wait_ge(norm_b, s.upto(1))
                reusable(act, s, lag, xn3_turned)
                if s.looped or s.kk - lag >= U:
                    act.wait_ge(xn3_kept[p], s.landed(lag + U))
                for j in range(J):
                    last = nc.scalar.activation(xn3[:, p, j], xs[:, g, j], ACT.Identity, bias=nb[:, q, J + j:J + j + 1],
                                                scale=rb[:, q, J + j:J + j + 1])
                last.then_inc(xn3_ready, 1)

            def step(s):
                norm3(s, 3)
                guess_a(s, -1)
                copy_turned(s, xn3_turned, xn3T, P, J * S, g_done)
                copy_turned(s, xn2_turned, xn2T, P, J * S, scores_done)
                copy_gate(s, 3)
                exponentials(s, 1)
                copy_turned(s, xn1_turned, xn1T, P, J * S, h_done)
                copy_turned(s, probs_turned, probsT, Q, J * S, att_done)
                guess_b(s)
                copy_mapped(s, 0)
                copy_turned(s, masked_turned, c_maskedT, P, J * Q, mapped_done, scores_done)

            run(act, step)
            act.wait_ge(gate_ready, NG)
            for n in range(NG // 2):
                v = gate[:, 2 * n:2 * n + 2, :, 0:D].rearrange("p g j d -> p (g j) d")
                nc.scalar.activation(v, v, ACT.Gelu_apprx_tanh).then_inc(gelu_ready, 1)

        @block.vector
        def _(dve):
            made = [0]

            def made_then_wait(ins):
                made[0] += 1
                ins.then_inc(setup_dve, 1)
                dve.wait_ge(setup_dve, made[0])

            nc.vector.memset(ones_bf[:], 1.0)
            made_then_wait(nc.vector.memset(bias_parts[:], 0.0))
            made_then_wait(nc.vector.memset(eps_col[:], EPS))
            nc.vector.memset(bout_parts[:], 0.0)
            made_then_wait(nc.vector.memset(decay_row[:], 1.0))
            dve.wait_ge(misc_loaded, 16 * 14)
            dve.wait_ge(w_loaded, 16 * 4)
            nc.vector.tensor_scalar(w_nat[:, 0], w_nat[:, 0], cols[:, 1:2], None, ALU.mult)
            made_then_wait(nc.vector.tensor_copy(mask_nat[:], mask_int[:]))
            dve.wait_ge(tanh_done, 1)
            made_then_wait(nc.vector.tensor_scalar(decay[:, 1:2], decay[:, 0:1], 0.5, 0.5, ALU.mult, ALU.add))
            made_then_wait(nc.vector.tensor_scalar(decay_row[:], decay_row[:], decay[:, 1:2], None, ALU.mult))
            nc.vector.memset(decay_row[:, :, 0], 0.0)
            for r in (0, 32, 64):
                row = slice(r, r + 1)
                made_then_wait(nc.vector.tensor_tensor(bias_row[row, 1], bias_row[row, 0], bias_row[row, 1], ALU.mult))
                v = bias_row[row, 1:3]
                made_then_wait(nc.vector.tensor_copy(bias_hi[row], v))
                if r:
                    made_then_wait(nc.vector.tensor_tensor(bias_rest[row], v, bias_hi[row], ALU.subtract))
                    made_then_wait(nc.vector.tensor_copy(bias_mid[row], bias_rest[row]))
                if r == 64:
                    made_then_wait(nc.vector.tensor_tensor(bias_rest[row], bias_rest[row], bias_mid[row], ALU.subtract))
                src = {0: bias_hi, 32: bias_mid, 64: bias_rest}[r]
                nc.vector.tensor_copy(bias_parts[row, 0], src[row, 0])
                made_then_wait(nc.vector.tensor_copy(bout_parts[row], src[row, 1].unsqueeze(1).broadcast_to([1, J, P])))
            for n, dst in enumerate((w_inT, w_outT, mapWT)):
                dve.wait_ge(setup_pe, n + 1)
                nc.vector.tensor_copy(dst[:, 0:P], tr[n % 2][:, 0:P]).then_inc(setup_copied, 1)
            dve.wait_ge(setup_pe, 4)
            nc.vector.tensor_copy(maskT[:], tr[1][0:Q, 0:B]).then_inc(setup_copied, 1)
            nc.vector.tensor_scalar(mask_tiny[:], tr[1][0:Q, 0:B], TINY, None, ALU.add).then_inc(setup_copied, 1)

            def newton(mv, y, t, r, n, p, lo, hi, chain, count, done):
                var, mean = mv[:, p, lo:hi, 1], mv[:, p, lo:hi, 0]
                y, t0, t1, r, n = y[:, p, lo:hi], t[:, p, 0, lo:hi], t[:, p, 1, lo:hi], r[:, p, lo:hi], n[:, p, lo:hi]
                nc.vector.scalar_tensor_tensor(t0, y, -0.5, y, ALU.mult, ALU.mult).then_inc(chain, 1)
                dve.wait_ge(chain, count + 1)
                nc.vector.scalar_tensor_tensor(t1, var, EPS, t0, ALU.add, ALU.mult).then_inc(chain, 1)
                dve.wait_ge(chain, count + 2)
                nc.vector.scalar_tensor_tensor(r, t1, 1.5, y, ALU.add, ALU.mult).then_inc(chain, 1)
                dve.wait_ge(chain, count + 3)
                nc.vector.scalar_tensor_tensor(n, mean, -1.0, r, ALU.mult, ALU.mult).then_inc(done, 1)

            def scan(s, lag):
                if not s.has(lag):
                    return
                dve.wait_ge(h_done, s.upto(lag))
                reusable(dve, s, lag, o_done)
                nc.vector.tensor_tensor_scan(yT[:, s.slot(lag)].rearrange("p j t -> p (j t)"),
                                             decay_row[:].rearrange("p j t -> p (j t)"),
                                             h_ps[:].rearrange("p j t -> p (j t)"), 0.0, ALU.mult,
                                             ALU.add).then_inc(y_ready, 1)

            def scale_attended(s, lag):
                if not s.has(lag):
                    return
                p = s.slot(lag)
                dve.wait_ge(att_done, s.upto(lag))
                nc.vector.reciprocal(inv[:, p].rearrange("p (h j) -> p h j", h=2),
                                     wide_view[:, :, :, D]).then_inc(inv_ready, 1)
                dve.wait_ge(inv_ready, s.upto(lag))
                nc.vector.tensor_tensor(att[:, p].rearrange("p (h j) d -> p h j d", h=2), wide_view[:, :, :, 0:D],
                                        inv[:, p].rearrange("p (h j) -> p h j", h=2).unsqueeze(3)
                                        .broadcast_to([P, 2, 2, D]), ALU.mult).then_inc(att_scaled, 1)

            def stats1(s, lag):
                if not s.has(lag):
                    return
                p = s.slot(lag)
                dve.wait_ge(x_loaded[p], s.landed(lag))
                for j in range(J):
                    last = nc.vector.bn_stats(bn1[:, p, j], x_in[:, p, j])
                last.then_inc(bn1_done, 1)

            def aggregate1(s, lag):
                if not s.has(lag):
                    return
                p = s.slot(lag)
                dve.wait_ge(bn1_done, s.upto(lag))
                apart(dve, s)
                for j in range(J):
                    last = nc.vector.bn_aggr(mva[:, p, j], bn1[:, p, j])
                last.then_inc(stats_a, 1)

            def stats2(s, lag):
                if not s.has(lag):
                    return
                dve.wait_ge(x1_ready, s.upto(lag))
                apart(dve, s)
                for j in range(J):
                    last = nc.vector.bn_stats(bn2[:, s.slot(lag), j], xs[:, s.group(lag), j])
                last.then_inc(bn2_done, 1)

            def stats3(s, lag):
                if not s.has(lag):
                    return
                dve.wait_ge(x2_ready, s.upto(lag))
                apart(dve, s)
                for j in range(J):
                    last = nc.vector.bn_stats(bn3[:, s.slot(lag), j], xs[:, s.group(lag), j])
                last.then_inc(bn3_done, 1)

            def aggregate23(s):
                if s.has(0):
                    dve.wait_ge(bn2_done, s.upto(0))
                    apart(dve, s)
                    for j in range(J):
                        last = nc.vector.bn_aggr(mvb[:, s.slot(0), j], bn2[:, s.slot(0), j])
                if s.has(2):
                    dve.wait_ge(bn3_done, s.upto(2))
                    apart(dve, s)
                    for j in range(J):
                        last = nc.vector.bn_aggr(mvb[:, s.slot(0), J + j], bn3[:, s.slot(2), j])
                if s.has(0) or s.has(2):
                    last.then_inc(stats_b, 1)

            def newton_1(s, lag):
                if s.has(lag):
                    dve.wait_ge(rs_a, s.upto(lag))
                    newton(mva, ya, ta, ra, na, s.slot(lag), 0, J, newton_a, s.upto(lag + 1, 3), norm_a)

            def newton_23(s):
                if s.has(0) or s.has(2):
                    lo, hi = (0 if s.has(0) else J), (2 * J if s.has(2) else J)
                    dve.wait_ge(rs_b, s.upto(0))
                    newton(mvb, yb, tb, rb, nb, s.slot(0), lo, hi, newton_b, s.upto(1, 3), norm_b)

            def sum_x1(s, lag):
                if not s.has(lag):
                    return
                dve.wait_ge(o_done, s.upto(lag))
                nc.vector.tensor_tensor(xs[:, s.group(lag)], o_ps[:], x_in[:, s.slot(lag)], ALU.add).then_inc(x1_ready, 1)

            def sum_x2(s, lag):
                if not s.has(lag):
                    return
                flat = xs[:, s.group(lag)].rearrange("p j d -> p (j d)")
                dve.wait_ge(att_ready, s.upto(lag))
                nc.vector.scalar_tensor_tensor(flat, att[:, s.slot(lag)].rearrange("p j d -> p (j d)"), 0.0, flat,
                                               ALU.max, ALU.add).then_inc(x2_ready, 1)

            def maximum(s, lag):
                if not s.has(lag):
                    return
                dve.wait_ge(scores_done, s.upto(lag))
                reusable(dve, s, lag, probs_ready)
                nc.vector.tensor_reduce(negmax[:, s.slot(lag)], s_view, AX_X, ALU.max, negate=True).then_inc(max_ready, 1)

            def step(s):
                scan(s, 0)
                stats1(s, -1)
                aggregate1(s, -1)
                scale_attended(s, 2)
                newton_1(s, -1)
                sum_x1(s, 0)
                stats2(s, 0)
                maximum(s, 1)
                sum_x2(s, 2)
                stats3(s, 2)
                aggregate23(s)
                newton_23(s)

            run(dve, step)

            dve.wait_ge(gate_ready, NG)
            nc.vector.tensor_copy(score[:].rearrange("p (g j) -> p g j", j=J), gate[:, :, :, D]).then_inc(score_ready, 1)
            dve.wait_ge(score_turned, 1)
            ranks = [0]

            def ranked_then_wait(ins):
                ranks[0] += 1
                ins.then_inc(rank_step, 1)
                dve.wait_ge(rank_step, ranks[0])

            ranked_then_wait(nc.vector.tensor_scalar(ranked[:], tr[0][0:B, 0:S], -1.0, None, ALU.mult))
            for _ in range(ROUNDS):
                ranked_then_wait(nc.vector.max(top8[:], ranked[:]))
                ranked_then_wait(nc.vector.match_replace(ranked[:], top8[:], ranked[:], LOWEST))
            ranked_then_wait(nc.vector.tensor_scalar(dropped[:, ::-1], ranked[:], LOWEST, None, ALU.is_equal))
            dve.wait_ge(dropped_turned, 1)
            ranked_then_wait(nc.vector.tensor_copy(droppedT[:], tr[1][:, 0:B]))
            for n in range(NG // 2):
                dve.wait_ge(gelu_ready, n + 1)
                if n == 0:
                    for q in range(U):
                        dve.wait_ge(xn3_kept[q], 16 * (NG // U))
                b0 = 2 * J * n
                nc.vector.copy_predicated(gate[:, 2 * n:2 * n + 2, :, 0:D].rearrange("p g j d -> p (g j) d"),
                                          droppedT[:, b0:b0 + 2 * J].bitcast(mybir.dt.uint32).unsqueeze(2)
                                          .broadcast_to([P, 2 * J, D]),
                                          xn3_all[:, 2 * n:2 * n + 2].rearrange("p g j d -> p (g j) d")).then_inc(picked, 1)

        @block.tensor
        def _(pe):
            pe.wait_ge(ident_made, 4)
            pe.wait_ge(setup_dve, 4)
            pe.wait_ge(w_loaded, 16 * 4)
            for n in range(3):
                if n >= 2:
                    pe.wait_ge(setup_copied, n - 1)
                nc.tensor.transpose(tr[n % 2][:, 0:P], w_nat[:, n], ident[:]).then_inc(setup_pe, 1)
            pe.wait_ge(setup_copied, 2)
            nc.tensor.transpose(tr[1][0:Q, 0:B], mask_nat[:], ident[0:B, 0:B]).then_inc(setup_pe, 1)
            pe.wait_ge(setup_copied, 5)

            def turn(s, turned, src, ready, rows, cols_):
                lag = TURNS[TURN_OF[turned]][0]
                if not s.has(lag):
                    return
                pe.wait_ge(ready, s.upto(lag))
                turn_free(pe, s, turned)
                dst = turn_bank(s, turned)
                for j in range(J):
                    last = nc.tensor.transpose(dst[0:cols_, j * rows:(j + 1) * rows], src[0:rows, s.slot(lag), j],
                                               ident[0:rows, 0:rows])
                last.then_inc(turned, 1)

            def input_product(s, lag):
                if not s.has(lag):
                    return
                pe.wait_ge(xn1T_ready, s.upto(lag))
                one_ago(pe, s, lag, y_ready)
                flat = h_ps[:].rearrange("p j t -> p (j t)")
                nc.tensor.matmul(flat, w_inT[:], xn1T[:, s.slot(lag)].rearrange("p j t -> p (j t)"), start=True, stop=False)
                nc.tensor.matmul(flat, bias_parts[:, 0], ones_bf[:], start=False, stop=True).then_inc(h_done, 1)

            def output_product(s, lag):
                if not s.has(lag):
                    return
                one_ago(pe, s, lag, x1_ready)
                flat = o_ps[:].rearrange("p j t -> p (j t)")
                nc.tensor.matmul(flat, ones_bf[:, 0:S], bout_parts[:].rearrange("p j d -> p (j d)"), start=True, stop=False)
                pe.wait_ge(y_ready, s.upto(lag))
                for j in range(J):
                    last = nc.tensor.matmul(o_ps[:, j], yT[:, s.slot(lag), j], w_outT[:], start=False, stop=(j == J - 1))
                last.then_inc(o_done, 1)

            def map_context(s, lag):
                if not s.has(lag):
                    return
                pe.wait_ge(maskedT_ready, s.upto(lag))
                one_ago(pe, s, lag, mapped_ready)
                for j in range(J):
                    last = nc.tensor.matmul(m_ps[0:Q, j], c_maskedT[:, s.slot(lag), j], mapWT[:], start=True, stop=True)
                last.then_inc(mapped_done, 1)

            def scores(s, lag):
                if not s.has(lag):
                    return
                pe.wait_ge(xn2T_ready, s.upto(lag))
                pe.wait_ge(maskedT_ready, s.upto(lag))
                one_ago(pe, s, lag, probs_ready)
                for j in range(J):
                    last = nc.tensor.matmul(s_view[:, j], xn2T[:, s.slot(lag), j], c_maskedT[:, s.slot(lag), j],
                                            start=True, stop=True)
                last.then_inc(scores_done, 1)

            def feed_forward(s, lag):
                if not s.has(lag):
                    return
                pe.wait_ge(xn3T_ready, s.upto(lag))
                if s.has(lag - 1):
                    pe.wait_ge(att_scaled, s.upto(lag - 1))
                else:
                    one_ago(pe, s, lag, gate_ready)
                for j in range(J):
                    last = nc.tensor.matmul(wide_view[:, j // 2, j % 2], xn3T[:, s.slot(lag), j], block_in[:],
                                            start=True, stop=True)
                last.then_inc(g_done, 1)

            def attend(s, lag):
                if not s.has(lag):
                    return
                pe.wait_ge(probsT_ready, s.upto(lag))
                pe.wait_ge(mapped_ready, s.upto(lag))
                pe.wait_ge(den_ready, s.upto(lag))
                if s.has(lag + 2):
                    pe.wait_ge(gate_ready, s.upto(lag + 2))
                else:
                    one_ago(pe, s, lag, att_scaled)
                for j in range(J):
                    last = nc.tensor.matmul(wide_view[:, j // 2, j % 2], probsT[:, s.slot(lag), j],
                                            c_mapped[:, s.slot(lag), j], start=True, stop=True)
                last.then_inc(att_done, 1)

            def step(s):
                output_product(s, 0)
                turn(s, xn3_turned, xn3, xn3_ready, P, D)
                turn(s, xn2_turned, xn2, xn2_ready, P, D)
                feed_forward(s, 3)
                scores(s, 1)
                map_context(s, 0)
                turn(s, xn1_turned, xn1, xn1_ready, P, D)
                turn(s, probs_turned, probs, probs_ready, P, Q)
                input_product(s, -1)
                turn(s, masked_turned, c_masked, masked_ready, Q, D)
                attend(s, 1)

            run(pe, step)
            pe.wait_ge(score_ready, 1)
            nc.tensor.transpose(tr[0][0:B, 0:S], score[:], flip[:]).then_inc(score_turned, 1)
            pe.wait_ge(rank_step, 2 * ROUNDS + 2)
            nc.tensor.transpose(tr[1][:, 0:B], dropped[:], ident[0:B, 0:B]).then_inc(dropped_turned, 1)


INPUTS = ["x", "ctx_1024", "mask_BxS2_ik0", "L0_attn_w_in", "L0_attn_b_in", "L0_attn_a", "L0_attn_b", "L0_attn_w_out",
          "L0_attn_b_out", "L0_xattn_map_W", "L0_xattn_map_b", "L0_ffn_w_router", "L0_ffn_w_block"]


def kernel(**inputs):
    import numpy as np
    import concourse.bacc as bacc
    from concourse.bass_utils import run_bass_kernel_spmd

    nc = bacc.Bacc("TRN2", target_bir_lowering=False, num_devices=1)
    arrays, args = {}, []
    for name in INPUTS:
        array = np.ascontiguousarray(inputs[name])
        arrays[f"in_{name}"] = array
        args.append(nc.dram_tensor(f"in_{name}", array.shape, mybir.dt.from_np(array.dtype), kind="ExternalInput").ap())
    out = nc.dram_tensor("out", inputs["x"].shape, F32, kind="ExternalOutput").ap()
    decoder_layer(nc, *args, out)
    result = run_bass_kernel_spmd(nc, [arrays], core_ids=[0])
    return result.results[0]["out"]
```

```python
from contextlib import ExitStack

import concourse.bass as bass
from concourse import mybir

F32 = mybir.dt.float32
BF16 = mybir.dt.bfloat16
I32 = mybir.dt.int32
ALU = mybir.AluOpType
ACT = mybir.ActivationFunctionType
AX_X = mybir.AxisListType.X

P = 128
J = 4
U = 2
EPS = 1e-5
TINY = 1e-13
LOWEST = -3.0e38
CAPACITY = 0.75


def decoder_layer(nc: bass.Bass, x, ctx, mask, w_in, b_in, a, b, w_out, b_out, map_W, map_b, w_router, w_block, out):
    B, S, D = x.shape
    Q = ctx.shape[1]
    NG = B // J
    DROP = S - max(1, int(S * CAPACITY))
    ROUNDS = DROP // 8
    CHAIN = 2 * ROUNDS + 1
    EARLY = NG - J
    PARTS = [(0, EARLY), (EARLY, NG)]
    assert S == P and D == P and B % (J * U) == 0 and DROP % 8 == 0
    FIRST, LAST = -2, NG + 2
    LOOP0, LOOP1 = 6, NG - 2
    assert (LOOP1 - LOOP0) % U == 0 and LOOP1 - LOOP0 > 0 and EARLY % 2 == 0

    x_dram = x.rearrange("(g j) t d -> g t j d", j=J)
    ctx_dram = ctx.rearrange("(g j) q d -> g q j d", j=J)
    out_dram = out.rearrange("(g j) t d -> g t j d", j=2 * J)

    with ExitStack() as stack:
        def sb(name, shape, dt=F32):
            return stack.enter_context(nc.sbuf_tensor(name, shape, dt))

        def ps(name, shape):
            return stack.enter_context(nc.psum_tensor(name, shape, F32))

        def sem(name):
            return stack.enter_context(nc.semaphore(name))

        ident = sb("ident", [P, P])
        flip = sb("flip", [P, P])
        w_nat = sb("w_nat", [P, 3, P])
        w_inT = sb("w_inT", [P, P])
        w_outT = sb("w_outT", [P, P])
        mapWT = sb("mapWT", [P, P])
        block_in = sb("block_in", [P, P + 1])
        cols = sb("cols", [P, 2])
        decay = sb("decay", [P, 2])
        decay_row = sb("decay_row", [P, J, S])
        mapb_all = sb("mapb_all", [P, P])
        eps_col = sb("eps_col", [P, 1])
        mask_int = sb("mask_int", [B, Q], I32)
        mask_nat = sb("mask_nat", [B, Q])
        maskT = sb("maskT", [Q, B])
        mask_tiny = sb("mask_tiny", [Q, B])
        bias_row = sb("bias_row", [65, 3, P])
        bias_rest = sb("bias_rest", [65, 2, P])
        bias_hi = sb("bias_hi", [65, 2, P], BF16)
        bias_mid = sb("bias_mid", [65, 2, P], BF16)
        bias_parts = sb("bias_parts", [65, 2, P], BF16)
        bout_parts = sb("bout_parts", [65, J, P], BF16)
        ones_bf = sb("ones_bf", [65, J * S], BF16)

        c_in = sb("c_in", [Q, U, J, D])
        c_masked = sb("c_masked", [Q, U, J, D])
        c_maskedT = sb("c_maskedT", [P, U, J, Q])
        xn1 = sb("xn1", [P, U, J, D])
        xn1T = sb("xn1T", [P, U, J, S])
        yT = sb("yT", [P, U, J, S])
        xn2 = sb("xn2", [P, U, J, D])
        xn2T = sb("xn2T", [P, U, J, S])
        probs = sb("probs", [P, U, J, Q])
        probsT = sb("probsT", [Q, U, J, S])
        c_mapped = sb("c_mapped", [Q, U, J, D + 1])
        att = sb("att", [P, U, J, D])
        xn3 = sb("xn3", [P, U, J, D])
        xn3T = sb("xn3T", [P, U, J, S])
        bn = sb("bn", [P, U, 3 * J, 6])
        mv = sb("mv", [P, U, 3 * J, 2])
        log_var = sb("log_var", [P, U, 3 * J])
        guessed = sb("guessed", [P, U, 3 * J])
        refining = sb("refining", [P, U, 2, 3 * J])
        rstd = sb("rstd", [P, U, 3 * J])
        shift = sb("shift", [P, U, 3 * J])
        negmax = sb("negmax", [P, U, J])
        inv = sb("inv", [P, U, J])

        xs = sb("xs", [P, NG, J, D])
        kept = sb("kept", [P, NG, J, D])
        gate = sb("gate", [P, NG, J, D + 1])
        score = sb("score", [P, B])
        ranked = sb("ranked", [B, 2, S])
        top8 = sb("top8", [B, 2, 8])
        dropped = sb("dropped", [B, 2, S])
        droppedT = sb("droppedT", [P, B])

        tr = [ps("tr0", [P, 512]), ps("tr1", [P, 512])]
        h_ps = ps("h_ps", [P, J, S])
        o_ps = ps("o_ps", [P, J, D])
        s_ps = ps("s_ps", [P, 512])
        m_ps = ps("m_ps", [P, J, D])
        wide = ps("wide", [P, 2, 512])
        s_view = s_ps[:, 0:J * Q].rearrange("p (j q) -> p j q", j=J)
        wide_view = wide[:, :, 0:2 * (D + 1)].rearrange("p h (j n) -> p h j n", j=2)

        ident_made = sem("ident_made")
        w_in_loaded = sem("w_in_loaded")
        a_loaded = sem("a_loaded")
        b_loaded = sem("b_loaded")
        mask_loaded = sem("mask_loaded")
        bias_loaded = sem("bias_loaded")
        w_out_loaded = sem("w_out_loaded")
        map_loaded = sem("map_loaded")
        mapb_loaded = sem("mapb_loaded")
        block_loaded = sem("block_loaded")
        setup_dve = sem("setup_dve")
        filled = sem("filled")
        w_in_scaled = sem("w_in_scaled")
        mask_cast = sem("mask_cast")
        bias_made = sem("bias_made")
        exp_done = sem("exp_done")
        w_in_turned = sem("w_in_turned")
        w_out_turned = sem("w_out_turned")
        map_turned = sem("map_turned")
        mask_turned = sem("mask_turned")
        w_in_copied = sem("w_in_copied")
        w_out_copied = sem("w_out_copied")
        map_copied = sem("map_copied")
        mask_copied = sem("mask_copied")
        x_loaded = [sem(f"x_loaded{s}") for s in range(U)]
        c_loaded = [sem(f"c_loaded{s}") for s in range(U)]
        bn1_done = sem("bn1_done")
        bn2_done = sem("bn2_done")
        bn3_done = sem("bn3_done")
        stats_1 = sem("stats_1")
        stats_2 = sem("stats_2")
        stats_3 = sem("stats_3")
        log_done = sem("log_done")
        guess_done = sem("guess_done")
        refined = sem("refined")
        norm_ready = sem("norm_ready")
        xn1_ready = sem("xn1_ready")
        xn1_turned = sem("xn1_turned")
        xn1T_ready = sem("xn1T_ready")
        h_done = sem("h_done")
        y_ready = sem("y_ready")
        o_done = sem("o_done")
        x1_ready = sem("x1_ready")
        masked_ready = sem("masked_ready")
        den_ready = sem("den_ready")
        masked_turned = sem("masked_turned")
        maskedT_ready = sem("maskedT_ready")
        mapped_done = sem("mapped_done")
        mapped_ready = sem("mapped_ready")
        xn2_centred = sem("xn2_centred")
        xn2_ready = sem("xn2_ready")
        xn2_turned = sem("xn2_turned")
        xn2T_ready = sem("xn2T_ready")
        scores_done = sem("scores_done")
        max_ready = sem("max_ready")
        probs_ready = sem("probs_ready")
        probs_turned = sem("probs_turned")
        probsT_ready = sem("probsT_ready")
        att_done = sem("att_done")
        inv_ready = sem("inv_ready")
        att_scaled = sem("att_scaled")
        att_ready = sem("att_ready")
        x2_ready = sem("x2_ready")
        xn3_ready = sem("xn3_ready")
        xn3_turned = sem("xn3_turned")
        xn3T_ready = sem("xn3T_ready")
        kept_ready = sem("kept_ready")
        g_done = sem("g_done")
        gate_ready = sem("gate_ready")
        score_ready = sem("score_ready")
        score_turned = sem("score_turned")
        rank_step = sem("rank_step")
        dropped_turned = sem("dropped_turned")
        drop_ready = sem("drop_ready")
        gelu_ready = sem("gelu_ready")
        picked = sem("picked")
        summed = sem("summed")
        summed_here = sem("summed_here")
        stored = sem("stored")

        class Step:
            def __init__(self, kk, i):
                self.kk, self.i = kk, i
                self.looped = not isinstance(i, int)

            def has(self, lag):
                return self.looped or 0 <= self.kk - lag < NG

            def slot(self, lag):
                return (self.kk - lag) % U

            def group(self, lag):
                return self.kk - lag + U * self.i

            def upto(self, lag, each=1):
                return each * (self.kk - lag + 1) + (each * U) * self.i

            def landed(self, lag):
                return 16 * ((self.kk - lag) // U + 1) + 16 * self.i

        def run(engine, start, step, finish):
            start()
            for kk in range(FIRST + 4, LOOP0):
                step(Step(kk, 0))
            with engine.Fori(0, (LOOP1 - LOOP0) // U) as i:
                for kk in range(LOOP0, LOOP0 + U):
                    step(Step(kk, i))
            finish()

        f1, f2, f3, f4 = (Step(kk, 0) for kk in range(FIRST, FIRST + 4))
        s1, s2, s3, s4, s5 = (Step(kk, 0) for kk in range(LOOP1, LAST + 1))

        LN1, LN2, LN3 = 0, J, 2 * J

        def columns(s, lag):
            has = [s.has(lag - 2), s.has(lag), s.has(lag + 2)]
            return (J * has.index(True), 3 * J - J * has[::-1].index(True)) if any(has) else None

        def sets(s, lag, each=1):
            return s.upto(lag, each) - FIRST * each

        def reusable(eng, s, lag, signal):
            if s.looped or s.kk - lag >= U:
                eng.wait_ge(signal, s.upto(lag + U))

        def apart(eng, s):
            if s.looped:
                eng.nop(nofuse=True)

        def one_ago(eng, s, lag, signal):
            if s.looped or s.kk - lag >= 1:
                eng.wait_ge(signal, s.upto(lag + 1))

        TURNS = [(1, xn2_turned, xn2T_ready),
                 (3, xn3_turned, xn3T_ready),
                 (-1, xn1_turned, xn1T_ready),
                 (1, probs_turned, probsT_ready),
                 (-1, masked_turned, maskedT_ready)]
        TURN_OF = {turned: n for n, (_, turned, _) in enumerate(TURNS)}

        def turn_bank(s, turned, lag):
            kk = s.kk - lag + TURNS[TURN_OF[turned]][0]
            return tr[(len(TURNS) * kk + TURN_OF[turned]) % 2]

        def turn_free(eng, s, turned):
            at = len(TURNS) * s.kk + TURN_OF[turned] - 2
            while at >= len(TURNS) * FIRST:
                kk, m = divmod(at, len(TURNS))
                lag, _, copied = TURNS[m]
                if s.looped or 0 <= kk - lag < NG:
                    eng.wait_ge(copied, Step(kk, s.i).upto(lag))
                    return
                at -= 2

        POOL_PAIRS = [0, 2, 4, 6]
        DVE_PAIRS = [n for n in range(NG // 2) if n not in POOL_PAIRS]

        def part_rows(part):
            return J * (PARTS[part][1] - PARTS[part][0])

        def add_stream(engine, n):
            return engine.tensor_tensor(result(n), result(n), stream(n), ALU.add)

        def result(n):
            return gate[:, 2 * n:2 * n + 2, :, 0:D].rearrange("p g j d -> p (g j) d")

        def stream(n):
            return xs[:, 2 * n:2 * n + 2].rearrange("p g j d -> p (g j) d")

        block = stack.enter_context(nc.Block())

        @block.sync
        def _(sp):
            def load_soon():
                sp.dma_start(mask_int[:], mask).then_inc(mask_loaded, 16)
                sp.wait_ge(filled, 1)
                for n, v in enumerate((b_in, b, b_out)):
                    sp.dma_start(bias_row[0:65:32, n, :], v.rearrange("(o d) -> o d", o=1).broadcast_to([3, D])).then_inc(bias_loaded, 16)
                sp.dma_start(cols[:, 0:1], a.rearrange("(d o) -> d o", o=1)).then_inc(a_loaded, 16)

            def load_later():
                sp.dma_start(w_nat[:, 1], w_out).then_inc(w_out_loaded, 16)
                sp.dma_start(w_nat[:, 2], map_W).then_inc(map_loaded, 16)
                sp.dma_start(mapb_all[:], map_b.rearrange("(o d) -> o d", o=1).broadcast_to([P, D])).then_inc(mapb_loaded, 16)
                sp.dma_start(block_in[:, 0:D], w_block).then_inc(block_loaded, 16)
                sp.dma_start(block_in[:, D:D + 1], w_router.rearrange("(d o) -> d o", o=1)).then_inc(block_loaded, 16)

            def load(s, lag):
                if s.has(lag):
                    g = s.group(lag)
                    reusable(sp, s, lag, bn1_done)
                    sp.dma_start(xs[:, g], x_dram[g]).then_inc(x_loaded[s.slot(lag)], 16)
                    reusable(sp, s, lag, masked_ready)
                    sp.dma_start(c_in[:, s.slot(lag)], ctx_dram[g]).then_inc(c_loaded[s.slot(lag)], 16)

            def start():
                load(f1, -2)
                load_soon()
                load(f2, -2)
                load_later()
                load(f3, -2)
                load(f4, -2)

            def step(s):
                load(s, -2)

            run(sp, start, step, lambda: None)
            for n in range(NG // 2):
                sp.wait_ge(picked, n + 1)
                sp.dma_start(out_dram[n], gate[:, 2 * n:2 * n + 2, :, 0:D]).then_inc(stored, 16)
            sp.wait_ge(stored, 16 * (NG // 2))

        @block.gpsimd
        def _(pool):
            nc.gpsimd.memset(bias_row[:], 0.0).then_inc(filled, 1)
            nc.gpsimd.memset(ident[:], 0.0).then_inc(ident_made, 1)
            nc.gpsimd.memset(flip[:], 0.0).then_inc(ident_made, 1)
            pool.wait_ge(ident_made, 2)
            nc.gpsimd.affine_select(out=ident[:], in_=ident[:], compare_op=ALU.not_equal, fill=1.0, base=0,
                                    pattern=[[-1, P]], channel_multiplier=1).then_inc(ident_made, 1)
            nc.gpsimd.affine_select(out=flip[:], in_=flip[:], compare_op=ALU.not_equal, fill=1.0, base=1 - P,
                                    pattern=[[1, P]], channel_multiplier=1).then_inc(ident_made, 1)

            nc.gpsimd.memset(ones_bf[:], 1.0).then_inc(filled, 1)
            nc.gpsimd.memset(bias_parts[:], 0.0).then_inc(filled, 1)
            nc.gpsimd.memset(bout_parts[:], 0.0).then_inc(filled, 1)
            nc.gpsimd.memset(decay_row[:], 1.0).then_inc(filled, 1)
            pool.wait_ge(w_in_loaded, 16)
            pool.wait_ge(b_loaded, 16)
            nc.gpsimd.tensor_scalar(w_nat[:, 0], w_nat[:, 0], cols[:, 1:2], None, ALU.mult).then_inc(w_in_scaled, 1)
            pool.wait_ge(mask_loaded, 16)
            nc.gpsimd.tensor_copy(mask_nat[:], mask_int[:]).then_inc(mask_cast, 1)

            def centre2(s, lag):
                if not s.has(lag):
                    return
                g, p = s.group(lag), s.slot(lag)
                pool.wait_ge(stats_2, s.upto(lag))
                reusable(pool, s, lag, xn2_turned)
                nc.gpsimd.tensor_tensor(xn2[:, p], xs[:, g], mv[:, p, LN2:LN2 + J, 0].unsqueeze(2).broadcast_to([P, J, D]),
                                        ALU.subtract).then_inc(xn2_centred, 1)

            def norm2(s, lag):
                if not s.has(lag):
                    return
                p = s.slot(lag)
                pool.wait_ge(norm_ready, sets(s, lag))
                pool.wait_ge(xn2_centred, s.upto(lag))
                nc.gpsimd.tensor_tensor(xn2[:, p], xn2[:, p], rstd[:, p, LN2:LN2 + J].unsqueeze(2).broadcast_to([P, J, D]),
                                        ALU.mult).then_inc(xn2_ready, 1)

            def mask_context(s, lag):
                if not s.has(lag):
                    return
                g, p = s.group(lag), s.slot(lag)
                mask_cols = maskT[:].rearrange("q (g j) -> q g j", j=J)[:, g]
                if not s.looped and s.kk == lag:
                    pool.wait_ge(mask_copied, 1)
                pool.wait_ge(c_loaded[p], s.landed(lag))
                reusable(pool, s, lag, masked_turned)
                nc.gpsimd.tensor_tensor(c_masked[:, p], c_in[:, p], mask_cols.unsqueeze(2).broadcast_to([Q, J, D]),
                                        ALU.mult).then_inc(masked_ready, 1)

            def sum_column(s, lag):
                if not s.has(lag):
                    return
                if not s.looped and s.kk == lag:
                    pool.wait_ge(mask_copied, 2)
                tiny_cols = mask_tiny[:].rearrange("q (g j) -> q g j", j=J)[:, s.group(lag)]
                reusable(pool, s, lag, att_done)
                nc.gpsimd.tensor_copy(c_mapped[:, s.slot(lag), :, D], tiny_cols).then_inc(den_ready, 1)

            def add_map_b(s, lag):
                if not s.has(lag):
                    return
                p = s.slot(lag)
                pool.wait_ge(att_scaled, s.upto(lag))
                if not s.looped and s.kk == lag:
                    pool.wait_ge(mapb_loaded, 16)
                nc.gpsimd.tensor_tensor(att[:, p], att[:, p], mapb_all[:].unsqueeze(1).broadcast_to([P, J, D]),
                                        ALU.add).then_inc(att_ready, 1)

            def keep(s, lag):
                if not s.has(lag):
                    return
                pool.wait_ge(xn3_ready, s.upto(lag))
                nc.gpsimd.tensor_tensor(kept[:, s.group(lag)], xs[:, s.group(lag)], xn3[:, s.slot(lag)],
                                        ALU.add).then_inc(kept_ready, 1)

            def sum_up(pair):
                pool.wait_ge(gelu_ready, pair + 1)
                add_stream(nc.gpsimd, pair).then_inc(summed, 1)

            def start():
                mask_context(f2, -1)
                sum_column(f3, 0)
                mask_context(f3, -1)
                centre2(f3, 0)
                norm2(f3, 0)
                sum_column(f4, 0)
                mask_context(f4, -1)
                centre2(f4, 0)
                norm2(f4, 0)

            def step(s):
                add_map_b(s, 2)
                keep(s, 3)
                sum_column(s, 0)
                mask_context(s, -1)
                centre2(s, 0)
                norm2(s, 0)

            def finish():
                add_map_b(s1, 2)
                keep(s1, 3)
                mask_context(s1, -1)
                sum_column(s1, 0)
                centre2(s1, 0)
                norm2(s1, 0)
                add_map_b(s2, 2)
                keep(s2, 3)
                sum_column(s2, 0)
                centre2(s2, 0)
                norm2(s2, 0)
                add_map_b(s3, 2)
                keep(s3, 3)
                add_map_b(s4, 2)
                keep(s4, 3)
                keep(s5, 3)
                sum_up(0)
                sum_up(2)
                sum_up(4)
                sum_up(6)

            run(pool, start, step, finish)
        @block.scalar
        def _(act):
            act.dma_start(w_nat[:, 0], w_in).then_inc(w_in_loaded, 16)
            act.dma_start(cols[:, 1:2], b.rearrange("(d o) -> d o", o=1)).then_inc(b_loaded, 16)
            nc.scalar.preload_act_table_set("natural_log_exp_and_others")
            act.wait_ge(setup_dve, 1)

            def exp_a():
                act.wait_ge(a_loaded, 16)
                nc.scalar.activation(decay[:, 0:1], cols[:, 0:1], ACT.Exp, scale=-1.0).then_inc(exp_done, 1)

            def copy_w_out():
                act.wait_ge(w_out_turned, 1)
                nc.scalar.activation(w_outT[:], o_ps[:, 0], ACT.Copy).then_inc(w_out_copied, 1)

            def copy_map_W():
                act.wait_ge(map_turned, 1)
                nc.scalar.activation(mapWT[:], wide[:, 0, 0:P], ACT.Copy).then_inc(map_copied, 1)

            def guess(s, lag):
                if not columns(s, lag):
                    return
                (lo, hi), p = columns(s, lag), s.slot(lag)
                for signal, behind in ((stats_1, lag - 2), (stats_2, lag), (stats_3, lag + 2)):
                    if s.has(behind):
                        act.wait_ge(signal, s.upto(behind))
                nc.scalar.activation(log_var[:, p, lo:hi], mv[:, p, lo:hi, 1], ACT.Ln, bias=eps_col[:, 0:1]).then_inc(log_done, 1)
                act.wait_ge(log_done, sets(s, lag))
                nc.scalar.activation(guessed[:, p, lo:hi], log_var[:, p, lo:hi], ACT.Exp, scale=-0.5).then_inc(guess_done, 1)

            def copy_turned(s, lag, turned, dst, rows, width, *used):
                copied = TURNS[TURN_OF[turned]][2]
                if not s.has(lag):
                    return
                act.wait_ge(turned, s.upto(lag))
                for signal in used:
                    reusable(act, s, lag, signal)
                nc.scalar.activation(dst[:, s.slot(lag)].rearrange("p j t -> p (j t)"),
                                     turn_bank(s, turned, lag)[0:rows, 0:width], ACT.Copy).then_inc(copied, 1)

            def exponentials(s, lag):
                if not s.has(lag):
                    return
                p = s.slot(lag)
                act.wait_ge(max_ready, s.upto(lag))
                reusable(act, s, lag, probs_turned)
                for j in range(J):
                    last = nc.scalar.activation(probs[:, p, j], s_view[:, j], ACT.Exp, bias=negmax[:, p, j:j + 1])
                last.then_inc(probs_ready, 1)

            def copy_gate(s, lag):
                if not s.has(lag):
                    return
                act.wait_ge(g_done, s.upto(lag))
                nc.scalar.activation(gate[:, s.group(lag)].rearrange("p (h j) n -> p h j n", h=2), wide_view,
                                     ACT.Copy).then_inc(gate_ready, 1)

            def copy_mapped(s, lag):
                if not s.has(lag):
                    return
                act.wait_ge(mapped_done, s.upto(lag))
                reusable(act, s, lag, att_done)
                nc.scalar.activation(c_mapped[:, s.slot(lag), :, 0:D], m_ps[0:Q], ACT.Copy).then_inc(mapped_ready, 1)

            def normalise(s, dst, first, lag, done):
                g, p = s.group(lag), s.slot(lag)
                for j in range(J):
                    c = first + j
                    last = nc.scalar.activation(dst[:, p, j], xs[:, g, j], ACT.Identity, bias=shift[:, p, c:c + 1],
                                                scale=rstd[:, p, c:c + 1])
                last.then_inc(done, 1)

            def norm1(s, lag):
                if s.has(lag):
                    act.wait_ge(norm_ready, sets(s, lag + 2))
                    reusable(act, s, lag, xn1_turned)
                    normalise(s, xn1, LN1, lag, xn1_ready)

            def norm3(s, lag):
                if s.has(lag):
                    act.wait_ge(norm_ready, sets(s, lag - 2))
                    reusable(act, s, lag, xn3_turned)
                    reusable(act, s, lag, kept_ready)
                    normalise(s, xn3, LN3, lag, xn3_ready)

            def gelu(pair):
                act.wait_ge(gate_ready, 2 * pair + 2)
                nc.scalar.activation(result(pair), result(pair), ACT.Gelu_apprx_tanh).then_inc(gelu_ready, 1)

            def start():
                guess(f1, 0)
                norm1(f2, -1)
                exp_a()
                copy_turned(f2, -1, xn1_turned, xn1T, P, J * S, h_done)
                guess(f2, 0)
                copy_turned(f2, -1, masked_turned, c_maskedT, P, J * Q, mapped_done, scores_done)
                copy_w_out()
                copy_map_W()
                norm1(f3, -1)
                copy_turned(f3, -1, xn1_turned, xn1T, P, J * S, h_done)
                copy_mapped(f3, 0)
                guess(f3, 0)
                copy_turned(f3, -1, masked_turned, c_maskedT, P, J * Q, mapped_done, scores_done)
                copy_turned(f3, 0, xn2_turned, xn2T, P, J * S, scores_done)
                norm1(f4, -1)
                exponentials(f4, 1)
                copy_turned(f4, -1, xn1_turned, xn1T, P, J * S, h_done)
                copy_mapped(f4, 0)
                copy_turned(f4, 1, probs_turned, probsT, Q, J * S, att_done)
                guess(f4, 0)
                copy_turned(f4, -1, masked_turned, c_maskedT, P, J * Q, mapped_done, scores_done)
                copy_turned(f4, 0, xn2_turned, xn2T, P, J * S, scores_done)

            def step(s):
                copy_turned(s, 3, xn3_turned, xn3T, P, J * S, g_done)
                norm1(s, -1)
                exponentials(s, 1)
                copy_turned(s, -1, xn1_turned, xn1T, P, J * S, h_done)
                copy_gate(s, 3)
                guess(s, 0)
                copy_turned(s, 1, probs_turned, probsT, Q, J * S, att_done)
                copy_mapped(s, 0)
                copy_turned(s, -1, masked_turned, c_maskedT, P, J * Q, mapped_done, scores_done)
                norm3(s, 2)
                copy_turned(s, 0, xn2_turned, xn2T, P, J * S, scores_done)

            def finish():
                copy_turned(s1, 3, xn3_turned, xn3T, P, J * S, g_done)
                norm1(s1, -1)
                exponentials(s1, 1)
                copy_turned(s1, -1, xn1_turned, xn1T, P, J * S, h_done)
                copy_turned(s1, 1, probs_turned, probsT, Q, J * S, att_done)
                guess(s1, 0)
                copy_gate(s1, 3)
                copy_turned(s1, -1, masked_turned, c_maskedT, P, J * Q, mapped_done, scores_done)
                norm3(s1, 2)
                copy_turned(s1, 0, xn2_turned, xn2T, P, J * S, scores_done)
                copy_mapped(s1, 0)
                copy_turned(s2, 3, xn3_turned, xn3T, P, J * S, g_done)
                exponentials(s2, 1)
                copy_mapped(s2, 0)
                copy_turned(s2, 1, probs_turned, probsT, Q, J * S, att_done)
                guess(s2, 0)
                copy_gate(s2, 3)
                norm3(s2, 2)
                copy_turned(s2, 0, xn2_turned, xn2T, P, J * S, scores_done)
                copy_turned(s3, 3, xn3_turned, xn3T, P, J * S, g_done)
                exponentials(s3, 1)
                copy_turned(s3, 1, probs_turned, probsT, Q, J * S, att_done)
                guess(s3, 0)
                copy_gate(s3, 3)
                norm3(s3, 2)
                copy_turned(s4, 3, xn3_turned, xn3T, P, J * S, g_done)
                guess(s4, 0)
                copy_gate(s4, 3)
                norm3(s4, 2)
                gelu(0)
                copy_turned(s5, 3, xn3_turned, xn3T, P, J * S, g_done)
                gelu(1)
                gelu(2)
                gelu(3)
                copy_gate(s5, 3)
                gelu(4)
                gelu(5)
                gelu(6)
                gelu(7)

            run(act, start, step, finish)
        @block.vector
        def _(dve):
            made = [0]

            def made_then_wait(ins):
                made[0] += 1
                ins.then_inc(setup_dve, 1)
                dve.wait_ge(setup_dve, made[0])

            made_then_wait(nc.vector.memset(eps_col[:], EPS))

            def copy_w_in():
                dve.wait_ge(w_in_turned, 1)
                nc.vector.tensor_copy(w_inT[:], m_ps[:, 0]).then_inc(w_in_copied, 1)

            def part_biases():
                v = bias_row[:, 1:3]
                dve.wait_ge(filled, 5)
                dve.wait_ge(bias_loaded, 16 * 3)
                made_then_wait(nc.vector.tensor_tensor(bias_row[:, 1], bias_row[:, 0], bias_row[:, 1], ALU.mult))
                made_then_wait(nc.vector.tensor_copy(bias_hi[:], v))
                made_then_wait(nc.vector.tensor_tensor(bias_rest[:], v, bias_hi[:], ALU.subtract))
                made_then_wait(nc.vector.tensor_copy(bias_mid[:], bias_rest[:]))
                made_then_wait(nc.vector.tensor_tensor(bias_rest[:], bias_rest[:], bias_mid[:], ALU.subtract))
                for r, part in ((0, bias_hi), (32, bias_mid), (64, bias_rest)):
                    nc.vector.tensor_copy(bias_parts[r:r + 1, 0], part[r:r + 1, 0])
                    last = nc.vector.tensor_copy(bout_parts[r:r + 1], part[r:r + 1, 1].unsqueeze(1).broadcast_to([1, J, P]))
                last.then_inc(bias_made, 1)

            def copy_mask():
                dve.wait_ge(mask_turned, 1)
                nc.vector.tensor_copy(maskT[:], s_ps[0:Q, 0:B]).then_inc(mask_copied, 1)
                nc.vector.tensor_scalar(mask_tiny[:], s_ps[0:Q, 0:B], TINY, None, ALU.add).then_inc(mask_copied, 1)

            def make_decay():
                dve.wait_ge(exp_done, 1)
                made_then_wait(nc.vector.tensor_scalar(decay[:, 0:1], decay[:, 0:1], 1.0, None, ALU.add))
                made_then_wait(nc.vector.reciprocal(decay[:, 1:2], decay[:, 0:1]))
                made_then_wait(nc.vector.tensor_scalar(decay_row[:], decay_row[:], decay[:, 1:2], None, ALU.mult))
                made_then_wait(nc.vector.memset(decay_row[:, :, 0], 0.0))

            def newton(s, lag, part):
                if not columns(s, lag):
                    return
                (lo, hi), p = columns(s, lag), s.slot(lag)
                mean, var = mv[:, p, lo:hi, 0], mv[:, p, lo:hi, 1]
                y, r, n = guessed[:, p, lo:hi], rstd[:, p, lo:hi], shift[:, p, lo:hi]
                t0, t1 = refining[:, p, 0, lo:hi], refining[:, p, 1, lo:hi]
                if part == 0:
                    dve.wait_ge(guess_done, sets(s, lag))
                    nc.vector.scalar_tensor_tensor(t0, y, -0.5, y, ALU.mult, ALU.mult).then_inc(refined, 1)
                    return
                dve.wait_ge(refined, sets(s, lag + 1, 3) + part)
                if part == 1:
                    nc.vector.scalar_tensor_tensor(t1, var, EPS, t0, ALU.add, ALU.mult).then_inc(refined, 1)
                elif part == 2:
                    nc.vector.scalar_tensor_tensor(r, t1, 1.5, y, ALU.add, ALU.mult).then_inc(refined, 1)
                else:
                    nc.vector.scalar_tensor_tensor(n, mean, -1.0, r, ALU.mult, ALU.mult).then_inc(norm_ready, 1)

            def scan(s, lag):
                if not s.has(lag):
                    return
                dve.wait_ge(h_done, s.upto(lag))
                reusable(dve, s, lag, o_done)
                nc.vector.tensor_tensor_scan(yT[:, s.slot(lag)].rearrange("p j t -> p (j t)"),
                                             decay_row[:].rearrange("p j t -> p (j t)"),
                                             h_ps[:].rearrange("p j t -> p (j t)"), 0.0, ALU.mult,
                                             ALU.add).then_inc(y_ready, 1)

            def invert(s, lag):
                if not s.has(lag):
                    return
                dve.wait_ge(att_done, s.upto(lag))
                nc.vector.reciprocal(inv[:, s.slot(lag)].rearrange("p (h j) -> p h j", h=2),
                                     wide_view[:, :, :, D]).then_inc(inv_ready, 1)

            def scale_attended(s, lag):
                if not s.has(lag):
                    return
                p = s.slot(lag)
                dve.wait_ge(inv_ready, s.upto(lag))
                nc.vector.tensor_tensor(att[:, p].rearrange("p (h j) d -> p h j d", h=2), wide_view[:, :, :, 0:D],
                                        inv[:, p].rearrange("p (h j) -> p h j", h=2).unsqueeze(3)
                                        .broadcast_to([P, 2, 2, D]), ALU.mult).then_inc(att_scaled, 1)

            def stats(s, lag, first, done):
                apart(dve, s)
                for j in range(J):
                    last = nc.vector.bn_stats(bn[:, s.slot(lag), first + j], xs[:, s.group(lag), j])
                last.then_inc(done, 1)

            def stats1(s, lag):
                if s.has(lag):
                    dve.wait_ge(x_loaded[s.slot(lag)], s.landed(lag))
                    stats(s, lag, LN1, bn1_done)

            def stats2(s, lag):
                if s.has(lag):
                    dve.wait_ge(x1_ready, s.upto(lag))
                    stats(s, lag, LN2, bn2_done)

            def stats3(s, lag):
                if s.has(lag):
                    dve.wait_ge(x2_ready, s.upto(lag))
                    stats(s, lag, LN3, bn3_done)

            def aggregate(s, lag, first, made, done):
                dve.wait_ge(made, s.upto(lag))
                apart(dve, s)
                for j in range(J):
                    last = nc.vector.bn_aggr(mv[:, s.slot(lag), first + j], bn[:, s.slot(lag), first + j])
                last.then_inc(done, 1)

            def aggregate1(s, lag):
                if s.has(lag):
                    aggregate(s, lag, LN1, bn1_done, stats_1)

            def aggregate2(s, lag):
                if s.has(lag):
                    reusable(dve, s, lag, xn2_centred)
                    aggregate(s, lag, LN2, bn2_done, stats_2)

            def aggregate3(s, lag):
                if s.has(lag):
                    aggregate(s, lag, LN3, bn3_done, stats_3)

            def sum_x1(s, lag):
                if not s.has(lag):
                    return
                dve.wait_ge(o_done, s.upto(lag))
                nc.vector.tensor_tensor(xs[:, s.group(lag)], o_ps[:], xs[:, s.group(lag)], ALU.add).then_inc(x1_ready, 1)

            def sum_x2(s, lag):
                if not s.has(lag):
                    return
                flat = xs[:, s.group(lag)].rearrange("p j d -> p (j d)")
                dve.wait_ge(att_ready, s.upto(lag))
                nc.vector.scalar_tensor_tensor(flat, att[:, s.slot(lag)].rearrange("p j d -> p (j d)"), 0.0, flat,
                                               ALU.max, ALU.add).then_inc(x2_ready, 1)

            def maximum(s, lag):
                if not s.has(lag):
                    return
                dve.wait_ge(scores_done, s.upto(lag))
                reusable(dve, s, lag, probs_ready)
                nc.vector.tensor_reduce(negmax[:, s.slot(lag)], s_view, AX_X, ALU.max, negate=True).then_inc(max_ready, 1)

            def gather(part):
                lo, hi = PARTS[part]
                dve.wait_ge(gate_ready, hi)
                nc.vector.tensor_scalar(score[:, J * lo:J * hi].rearrange("p (g j) -> p g j", j=J), gate[:, lo:hi, :, D],
                                        -1.0, None, ALU.mult).then_inc(score_ready, 1)

            def rank(part, lo, hi):
                rows = part_rows(part)
                top, target = top8[0:rows, part], ranked[0:rows, part]
                for n in range(lo, hi):
                    source = target if n > 1 else h_ps[0:rows, 2 * part]
                    if n == 0:
                        dve.wait_ge(score_turned, part + 1)
                    else:
                        dve.wait_ge(rank_step, CHAIN * part + n)
                    if n == CHAIN - 1:
                        last = nc.vector.tensor_scalar(dropped[0:rows, part, ::-1], target, LOWEST, None, ALU.is_equal)
                    elif n % 2 == 0:
                        last = nc.vector.max(top, source)
                    else:
                        last = nc.vector.match_replace(target, top, source, LOWEST)
                    last.then_inc(rank_step, 1)

            def pick_rows(part):
                lo, hi = PARTS[part]
                dve.wait_ge(dropped_turned, part + 1)
                nc.vector.tensor_copy(droppedT[:, J * lo:J * hi], h_ps[:, 2 * part + 1, 0:part_rows(part)]).then_inc(drop_ready, 1)

            def sum_up(pair):
                dve.wait_ge(gelu_ready, pair + 1)
                add_stream(nc.vector, pair).then_inc(summed_here, 1)

            def pick(pair):
                dve.wait_ge(drop_ready, 1 if 2 * pair < EARLY else 2)
                if pair in POOL_PAIRS:
                    dve.wait_ge(summed, POOL_PAIRS.index(pair) + 1)
                else:
                    dve.wait_ge(summed_here, DVE_PAIRS.index(pair) + 1)
                dve.wait_ge(kept_ready, 2 * pair + 2)
                b0 = 2 * J * pair
                nc.vector.copy_predicated(result(pair), droppedT[:, b0:b0 + 2 * J].bitcast(mybir.dt.uint32).unsqueeze(2)
                                          .broadcast_to([P, 2 * J, D]),
                                          kept[:, 2 * pair:2 * pair + 2].rearrange("p g j d -> p (g j) d")).then_inc(picked, 1)

            def start():
                stats1(f1, -2)
                aggregate1(f1, -2)
                newton(f1, 0, 0)
                newton(f1, 0, 1)
                newton(f1, 0, 2)
                newton(f1, 0, 3)
                copy_w_in()
                copy_mask()
                part_biases()
                make_decay()
                stats1(f2, -2)
                aggregate1(f2, -2)
                newton(f2, 0, 0)
                newton(f2, 0, 1)
                newton(f2, 0, 2)
                newton(f2, 0, 3)
                scan(f2, -1)
                stats1(f3, -2)
                aggregate1(f3, -2)
                sum_x1(f3, 0)
                stats2(f3, 0)
                aggregate2(f3, 0)
                newton(f3, 0, 0)
                newton(f3, 0, 1)
                newton(f3, 0, 2)
                newton(f3, 0, 3)
                scan(f3, -1)
                stats1(f4, -2)
                aggregate1(f4, -2)
                sum_x1(f4, 0)
                maximum(f4, 1)
                stats2(f4, 0)
                aggregate2(f4, 0)
                newton(f4, 0, 0)
                newton(f4, 0, 1)
                newton(f4, 0, 2)
                newton(f4, 0, 3)
                scan(f4, -1)

            def step(s):
                invert(s, 2)
                scale_attended(s, 2)
                stats1(s, -2)
                aggregate1(s, -2)
                sum_x2(s, 2)
                sum_x1(s, 0)
                maximum(s, 1)
                stats3(s, 2)
                stats2(s, 0)
                aggregate3(s, 2)
                aggregate2(s, 0)
                newton(s, 0, 0)
                newton(s, 0, 1)
                newton(s, 0, 2)
                newton(s, 0, 3)
                scan(s, -1)

            def finish():
                invert(s1, 2)
                scale_attended(s1, 2)
                sum_x2(s1, 2)
                sum_x1(s1, 0)
                maximum(s1, 1)
                stats3(s1, 2)
                stats2(s1, 0)
                aggregate3(s1, 2)
                aggregate2(s1, 0)
                newton(s1, 0, 0)
                newton(s1, 0, 1)
                newton(s1, 0, 2)
                newton(s1, 0, 3)
                scan(s1, -1)
                invert(s2, 2)
                scale_attended(s2, 2)
                sum_x2(s2, 2)
                sum_x1(s2, 0)
                maximum(s2, 1)
                stats3(s2, 2)
                stats2(s2, 0)
                aggregate3(s2, 2)
                aggregate2(s2, 0)
                gather(0)
                newton(s2, 0, 0)
                newton(s2, 0, 1)
                newton(s2, 0, 2)
                newton(s2, 0, 3)
                invert(s3, 2)
                scale_attended(s3, 2)
                maximum(s3, 1)
                sum_x2(s3, 2)
                stats3(s3, 2)
                aggregate3(s3, 2)
                newton(s3, 0, 0)
                rank(0, 0, 3)
                newton(s3, 0, 1)
                newton(s3, 0, 2)
                newton(s3, 0, 3)
                rank(0, 3, 6)
                invert(s4, 2)
                scale_attended(s4, 2)
                sum_x2(s4, 2)
                stats3(s4, 2)
                aggregate3(s4, 2)
                newton(s4, 0, 0)
                newton(s4, 0, 1)
                newton(s4, 0, 2)
                newton(s4, 0, 3)
                rank(0, 6, CHAIN)
                pick_rows(0)
                sum_up(1)
                pick(0)
                pick(1)
                sum_up(3)
                gather(1)
                pick(2)
                rank(1, 0, 1)
                pick(3)
                rank(1, 1, 2)
                rank(1, 2, 3)
                sum_up(5)
                rank(1, 3, 4)
                rank(1, 4, 5)
                pick(4)
                rank(1, 5, 6)
                rank(1, 6, 7)
                pick(5)
                rank(1, 7, CHAIN)
                sum_up(7)
                pick_rows(1)
                pick(6)
                pick(7)

            run(dve, start, step, finish)

        @block.tensor
        def _(pe):
            def turn_w_in():
                pe.wait_ge(ident_made, 4)
                pe.wait_ge(w_in_scaled, 1)
                nc.tensor.transpose(m_ps[:, 0], w_nat[:, 0], ident[:]).then_inc(w_in_turned, 1)

            def turn_mask():
                pe.wait_ge(mask_cast, 1)
                nc.tensor.transpose(s_ps[0:Q, 0:B], mask_nat[:], ident[0:B, 0:B]).then_inc(mask_turned, 1)

            def turn_w_out():
                pe.wait_ge(w_out_loaded, 16)
                nc.tensor.transpose(o_ps[:, 0], w_nat[:, 1], ident[:]).then_inc(w_out_turned, 1)

            def turn_map_W():
                pe.wait_ge(map_loaded, 16)
                nc.tensor.transpose(wide[:, 0, 0:P], w_nat[:, 2], ident[:]).then_inc(map_turned, 1)

            def turn(s, lag, turned, src, ready, rows, cols_):
                if not s.has(lag):
                    return
                pe.wait_ge(ready, s.upto(lag))
                turn_free(pe, s, turned)
                dst = turn_bank(s, turned, lag)
                for j in range(J):
                    last = nc.tensor.transpose(dst[0:cols_, j * rows:(j + 1) * rows], src[0:rows, s.slot(lag), j],
                                               ident[0:rows, 0:rows])
                last.then_inc(turned, 1)

            def input_product(s, lag):
                if not s.has(lag):
                    return
                pe.wait_ge(xn1T_ready, s.upto(lag))
                one_ago(pe, s, lag, y_ready)
                if not s.looped and s.kk == lag:
                    pe.wait_ge(w_in_copied, 1)
                    pe.wait_ge(bias_made, 1)
                flat = h_ps[:].rearrange("p j t -> p (j t)")
                nc.tensor.matmul(flat, w_inT[:], xn1T[:, s.slot(lag)].rearrange("p j t -> p (j t)"), start=True, stop=False)
                nc.tensor.matmul(flat, bias_parts[:, 0], ones_bf[:], start=False, stop=True).then_inc(h_done, 1)

            def output_product(s, lag):
                if not s.has(lag):
                    return
                one_ago(pe, s, lag, x1_ready)
                if not s.looped and s.kk == lag:
                    pe.wait_ge(bias_made, 1)
                    pe.wait_ge(w_out_copied, 1)
                flat = o_ps[:].rearrange("p j t -> p (j t)")
                nc.tensor.matmul(flat, ones_bf[:, 0:S], bout_parts[:].rearrange("p j d -> p (j d)"), start=True, stop=False)
                pe.wait_ge(y_ready, s.upto(lag))
                for j in range(J):
                    last = nc.tensor.matmul(o_ps[:, j], yT[:, s.slot(lag), j], w_outT[:], start=False, stop=(j == J - 1))
                last.then_inc(o_done, 1)

            def map_context(s, lag):
                if not s.has(lag):
                    return
                pe.wait_ge(maskedT_ready, s.upto(lag))
                one_ago(pe, s, lag, mapped_ready)
                if not s.looped and s.kk == lag:
                    pe.wait_ge(w_in_copied, 1)
                    pe.wait_ge(map_copied, 1)
                for j in range(J):
                    last = nc.tensor.matmul(m_ps[0:Q, j], c_maskedT[:, s.slot(lag), j], mapWT[:], start=True, stop=True)
                last.then_inc(mapped_done, 1)

            def scores(s, lag):
                if not s.has(lag):
                    return
                pe.wait_ge(xn2T_ready, s.upto(lag))
                pe.wait_ge(maskedT_ready, s.upto(lag))
                one_ago(pe, s, lag, probs_ready)
                if not s.looped and s.kk == lag:
                    pe.wait_ge(mask_copied, 2)
                for j in range(J):
                    last = nc.tensor.matmul(s_view[:, j], xn2T[:, s.slot(lag), j], c_maskedT[:, s.slot(lag), j],
                                            start=True, stop=True)
                last.then_inc(scores_done, 1)

            def feed_forward(s, lag):
                if not s.has(lag):
                    return
                pe.wait_ge(xn3T_ready, s.upto(lag))
                if not s.looped and s.kk == lag:
                    pe.wait_ge(block_loaded, 32)
                if s.has(lag - 1):
                    pe.wait_ge(att_scaled, s.upto(lag - 1))
                else:
                    one_ago(pe, s, lag, gate_ready)
                for j in range(J):
                    last = nc.tensor.matmul(wide_view[:, j // 2, j % 2], xn3T[:, s.slot(lag), j], block_in[:],
                                            start=True, stop=True)
                last.then_inc(g_done, 1)

            def attend(s, lag):
                if not s.has(lag):
                    return
                pe.wait_ge(probsT_ready, s.upto(lag))
                pe.wait_ge(mapped_ready, s.upto(lag))
                pe.wait_ge(den_ready, s.upto(lag))
                if not s.looped and s.kk == lag:
                    pe.wait_ge(map_copied, 1)
                if s.has(lag + 2):
                    pe.wait_ge(gate_ready, s.upto(lag + 2))
                else:
                    one_ago(pe, s, lag, att_scaled)
                for j in range(J):
                    last = nc.tensor.matmul(wide_view[:, j // 2, j % 2], probsT[:, s.slot(lag), j],
                                            c_mapped[:, s.slot(lag), j], start=True, stop=True)
                last.then_inc(att_done, 1)

            def turn_scores(part):
                lo, hi = PARTS[part]
                pe.wait_ge(score_ready, part + 1)
                pe.wait_ge(y_ready, NG)
                nc.tensor.transpose(h_ps[0:part_rows(part), 2 * part], score[:, J * lo:J * hi], flip[:]).then_inc(score_turned, 1)

            def turn_dropped(part):
                rows = part_rows(part)
                pe.wait_ge(rank_step, CHAIN * (part + 1))
                nc.tensor.transpose(h_ps[:, 2 * part + 1, 0:rows], dropped[0:rows, part],
                                    ident[0:rows, 0:rows]).then_inc(dropped_turned, 1)

            def start():
                turn_w_in()
                turn_mask()
                turn(f2, -1, xn1_turned, xn1, xn1_ready, P, D)
                turn(f2, -1, masked_turned, c_masked, masked_ready, Q, D)
                input_product(f2, -1)
                turn_w_out()
                turn_map_W()
                output_product(f3, 0)
                map_context(f3, 0)
                turn(f3, -1, xn1_turned, xn1, xn1_ready, P, D)
                turn(f3, -1, masked_turned, c_masked, masked_ready, Q, D)
                input_product(f3, -1)
                turn(f4, 1, xn2_turned, xn2, xn2_ready, P, D)
                output_product(f4, 0)
                scores(f4, 1)
                map_context(f4, 0)
                turn(f4, -1, xn1_turned, xn1, xn1_ready, P, D)
                turn(f4, 1, probs_turned, probs, probs_ready, P, Q)
                turn(f4, -1, masked_turned, c_masked, masked_ready, Q, D)
                input_product(f4, -1)

            def step(s):
                attend(s, 2)
                output_product(s, 0)
                turn(s, 1, xn2_turned, xn2, xn2_ready, P, D)
                turn(s, 3, xn3_turned, xn3, xn3_ready, P, D)
                scores(s, 1)
                map_context(s, 0)
                turn(s, -1, xn1_turned, xn1, xn1_ready, P, D)
                feed_forward(s, 3)
                turn(s, 1, probs_turned, probs, probs_ready, P, Q)
                turn(s, -1, masked_turned, c_masked, masked_ready, Q, D)
                input_product(s, -1)

            def finish():
                attend(s1, 2)
                turn(s1, 1, xn2_turned, xn2, xn2_ready, P, D)
                turn(s1, 3, xn3_turned, xn3, xn3_ready, P, D)
                output_product(s1, 0)
                scores(s1, 1)
                map_context(s1, 0)
                turn(s1, -1, xn1_turned, xn1, xn1_ready, P, D)
                feed_forward(s1, 3)
                turn(s1, 1, probs_turned, probs, probs_ready, P, Q)
                turn(s1, -1, masked_turned, c_masked, masked_ready, Q, D)
                input_product(s1, -1)
                attend(s2, 2)
                turn(s2, 1, xn2_turned, xn2, xn2_ready, P, D)
                turn(s2, 3, xn3_turned, xn3, xn3_ready, P, D)
                output_product(s2, 0)
                scores(s2, 1)
                map_context(s2, 0)
                turn(s2, 1, probs_turned, probs, probs_ready, P, Q)
                feed_forward(s2, 3)
                attend(s3, 2)
                turn(s3, 1, xn2_turned, xn2, xn2_ready, P, D)
                turn(s3, 3, xn3_turned, xn3, xn3_ready, P, D)
                scores(s3, 1)
                feed_forward(s3, 3)
                turn(s3, 1, probs_turned, probs, probs_ready, P, Q)
                turn_scores(0)
                attend(s4, 2)
                turn(s4, 3, xn3_turned, xn3, xn3_ready, P, D)
                feed_forward(s4, 3)
                turn_dropped(0)
                turn(s5, 3, xn3_turned, xn3, xn3_ready, P, D)
                feed_forward(s5, 3)
                turn_scores(1)
                turn_dropped(1)

            run(pe, start, step, finish)


INPUTS = ["x", "ctx_1024", "mask_BxS2_ik0", "L0_attn_w_in", "L0_attn_b_in", "L0_attn_a", "L0_attn_b", "L0_attn_w_out",
          "L0_attn_b_out", "L0_xattn_map_W", "L0_xattn_map_b", "L0_ffn_w_router", "L0_ffn_w_block"]


def kernel(**inputs):
    import numpy as np
    import concourse.bacc as bacc
    from concourse.bass_utils import run_bass_kernel_spmd

    nc = bacc.Bacc("TRN2", target_bir_lowering=False, num_devices=1)
    arrays, args = {}, []
    for name in INPUTS:
        array = np.ascontiguousarray(inputs[name])
        arrays[f"in_{name}"] = array
        args.append(nc.dram_tensor(f"in_{name}", array.shape, mybir.dt.from_np(array.dtype), kind="ExternalInput").ap())
    out = nc.dram_tensor("out", inputs["x"].shape, F32, kind="ExternalOutput").ap()
    decoder_layer(nc, *args, out)
    result = run_bass_kernel_spmd(nc, [arrays], core_ids=[0])
    return result.results[0]["out"]
```
